# Optimizing a Trainium2 kernel written in Bass

```python
import numpy as np
import jax
import jax.numpy as jnp

def _softmax(x, axis=-1):
    return jax.nn.softmax(x, axis=axis)

def _gelu(x):
    return jax.nn.gelu(x, approximate=True)

def _silu(x):
    return jax.nn.silu(x)

def _sigmoid(x):
    return jax.nn.sigmoid(x)

def _layernorm(x, axis=-1, eps=1e-05):
    m = jnp.mean(x, axis=axis, keepdims=True)
    v = jnp.var(x, axis=axis, keepdims=True)
    return (x - m) / jnp.sqrt(v + eps)

def _scatter_add(tgt, idx, src, axis=0):
    return tgt.at[idx].add(src)

def _segment_sum(src, seg, n):
    return jax.ops.segment_sum(src, seg, n)
kernel_name = 'mk_xattn_ffn_d1_seqx_r2_a51e40'

def setup_inputs(seed: int=0):
    np.random.seed(seed)
    _w = jnp.asarray

    def _rec_inputs():
        import jax
        import jax.numpy as jnp
        _rk = jax.random.key(seed)
        x = 7.22e-05 + 1 * jax.random.normal(jax.random.fold_in(_rk, 1), (16, 256, 512), jnp.float32)
        _lenS = 256 - jax.random.randint(jax.random.fold_in(_rk, 7), (16,), 0, max(1, 256 // 4) + 1, jnp.int32)
        _lenS2 = 256 - jax.random.randint(jax.random.fold_in(_rk, 8), (16,), 0, max(1, 256 // 4) + 1, jnp.int32)
        _ctx_1024P = jax.random.normal(jax.random.fold_in(_rk, 11), (16, 16, 512), jnp.float32)
        _ctx_1024c = jax.random.dirichlet(jax.random.fold_in(_rk, 511), 0.3 * jnp.ones((16,), jnp.float32), (16, 256))
        _ctx_1024t = jnp.einsum('bsk,bkd->bsd', _ctx_1024c, _ctx_1024P)
        _ctx_1024t = _ctx_1024t * jax.lax.rsqrt(jnp.mean(jnp.square(_ctx_1024t)) + 1e-12) * 0.953939
        ctx_1024 = 4.13588e-05 + 0.999923 * (_ctx_1024t + 0.3 * jax.random.normal(jax.random.fold_in(_rk, 611), (16, 256, 512), jnp.float32))
        return (x, ctx_1024)
    x, ctx_1024 = _rec_inputs()

    def _L0_xattn_setup():
        import jax, jax.numpy as jnp
        import numpy as np
        import math
        B, S, D, H = (4, 1024, 512, 16)
        HD = D // H

        def _rope_tables(seq_len, dim, base=10000.0):
            half = dim // 2
            inv_freq = 1.0 / base ** (jnp.arange(half, dtype=jnp.float32) / half)
            angles = jnp.arange(seq_len, dtype=jnp.float32)[:, None] * inv_freq[None, :]
            return (jnp.cos(angles), jnp.sin(angles))

        def _apply_rope(x, cos, sin):
            half = x.shape[-1] // 2
            x1, x2 = (x[..., :half], x[..., half:])
            c = cos[None, None, :, :]
            s = sin[None, None, :, :]
            return jnp.concatenate([x1 * c - x2 * s, x1 * s + x2 * c], axis=-1)
        key = jax.random.key(seed)
        ks = jax.random.split(key, 7)
        sc = 1.0 / math.sqrt(D)
        return {'Q': jax.random.normal(ks[0], (B, S, D), jnp.float32), 'K': jax.random.normal(ks[1], (B, S, D), jnp.float32), 'V': jax.random.normal(ks[2], (B, S, D), jnp.float32), 'Wq': jax.random.normal(ks[3], (D, D), jnp.float32) * sc, 'bq': jnp.zeros((D,), jnp.float32), 'Wk': jax.random.normal(ks[4], (D, D), jnp.float32) * sc, 'bk': jnp.zeros((D,), jnp.float32), 'Wv': jax.random.normal(ks[5], (D, D), jnp.float32) * sc, 'bv': jnp.zeros((D,), jnp.float32), 'Wo': jax.random.normal(ks[6], (D, D), jnp.float32) * sc, 'bo': jnp.zeros((D,), jnp.float32)}
    _L0_xattn_all = _L0_xattn_setup()
    _L0_xattn_in = {k: v for k, v in _L0_xattn_all.items() if k in ('Wq', 'bq', 'Wk', 'bk', 'Wv', 'bv', 'Wo', 'bo')}
    del _L0_xattn_all

    def _L0_ffn_setup():
        import jax, jax.numpy as jnp
        import numpy as np
        BLOCK = 32
        W_BITS = 4
        ACT_BITS = 16

        def act_qdq(x):
            qmax = 2.0 ** (ACT_BITS - 1) - 1.0
            scale = jnp.maximum(jnp.max(jnp.abs(x)) / qmax, 1e-12)
            return jnp.clip(jnp.round(x / scale), -qmax - 1.0, qmax) * scale

        def fixed_qdq_u16(x):
            scale = 1.0 / 65536.0
            return jnp.clip(jnp.round(x / scale), 0.0, 65535.0) * scale

        def lpbq_dequant(w):
            O, I = w.shape
            qmax = 2.0 ** (W_BITS - 1) - 1.0
            wb = w.reshape(O, I // BLOCK, BLOCK)
            s = jnp.maximum(jnp.max(jnp.abs(wb), axis=-1, keepdims=True) / qmax, 1e-12)
            wq = jnp.clip(jnp.round(wb / s), -qmax - 1.0, qmax) * s
            return wq.reshape(O, I)
        key = jax.random.key(seed)
        k1, k2, k3, k4 = jax.random.split(key, 4)
        B, S, H, I = (2, 2048, 512, 1536)
        x = jax.random.normal(k1, (B, S, H), jnp.float32)
        w_gate = jax.random.normal(k2, (I, H), jnp.float32) * 0.02
        w_up = jax.random.normal(k3, (I, H), jnp.float32) * 0.02
        w_down = jax.random.normal(k4, (H, I), jnp.float32) * 0.02
        return {'x': x, 'w_gate': w_gate, 'w_up': w_up, 'w_down': w_down}
    _L0_ffn_all = _L0_ffn_setup()
    _L0_ffn_in = {k: v for k, v in _L0_ffn_all.items() if k in ('w_gate', 'w_up', 'w_down')}
    del _L0_ffn_all
    return {'x': x, 'ctx_1024': ctx_1024, 'L0_xattn_Wq': _L0_xattn_in['Wq'], 'L0_xattn_bq': _L0_xattn_in['bq'], 'L0_xattn_Wk': _L0_xattn_in['Wk'], 'L0_xattn_bk': _L0_xattn_in['bk'], 'L0_xattn_Wv': _L0_xattn_in['Wv'], 'L0_xattn_bv': _L0_xattn_in['bv'], 'L0_xattn_Wo': _L0_xattn_in['Wo'], 'L0_xattn_bo': _L0_xattn_in['bo'], 'L0_ffn_w_gate': _L0_ffn_in['w_gate'], 'L0_ffn_w_up': _L0_ffn_in['w_up'], 'L0_ffn_w_down': _L0_ffn_in['w_down']}

def reference(x, ctx_1024, L0_xattn_Wq, L0_xattn_bq, L0_xattn_Wk, L0_xattn_bk, L0_xattn_Wv, L0_xattn_bv, L0_xattn_Wo, L0_xattn_bo, L0_ffn_w_gate, L0_ffn_w_up, L0_ffn_w_down):
    import jax
    import jax.numpy as jnp

    def _L0_xattn_ref(Q, K, V, Wq, bq, Wk, bk, Wv, bv, Wo, bo):
        import jax, jax.numpy as jnp
        import numpy as np
        import math
        B, S, D, H = (4, 1024, 512, 16)
        HD = D // H

        def _rope_tables(seq_len, dim, base=10000.0):
            half = dim // 2
            inv_freq = 1.0 / base ** (jnp.arange(half, dtype=jnp.float32) / half)
            angles = jnp.arange(seq_len, dtype=jnp.float32)[:, None] * inv_freq[None, :]
            return (jnp.cos(angles), jnp.sin(angles))

        def _apply_rope(x, cos, sin):
            half = x.shape[-1] // 2
            x1, x2 = (x[..., :half], x[..., half:])
            c = cos[None, None, :, :]
            s = sin[None, None, :, :]
            return jnp.concatenate([x1 * c - x2 * s, x1 * s + x2 * c], axis=-1)
        bs, n, _ = Q.shape
        q = (Q @ Wq.T + bq).reshape(bs, n, H, HD).transpose(0, 2, 1, 3)
        k = (K @ Wk.T + bk).reshape(bs, n, H, HD).transpose(0, 2, 1, 3)
        v = (V @ Wv.T + bv).reshape(bs, n, H, HD).transpose(0, 2, 1, 3)
        cos, sin = _rope_tables(n, HD)
        q = _apply_rope(q, cos, sin)
        k = _apply_rope(k, cos, sin)
        scores = jnp.einsum('bhqd,bhkd->bhqk', q, k) / math.sqrt(HD)
        causal = jnp.tril(jnp.ones((n, n), dtype=bool))
        scores = jnp.where(causal[None, None], scores, -jnp.inf)
        probs = jax.nn.softmax(scores, axis=-1)
        out = jnp.einsum('bhqk,bhkd->bhqd', probs, v)
        out = out.transpose(0, 2, 1, 3).reshape(bs, n, D)
        return out @ Wo.T + bo

    def _L0_ffn_ref(x, w_gate, w_up, w_down):
        import jax, jax.numpy as jnp
        import numpy as np
        BLOCK = 32
        W_BITS = 4
        ACT_BITS = 16

        def act_qdq(x):
            qmax = 2.0 ** (ACT_BITS - 1) - 1.0
            scale = jnp.maximum(jnp.max(jnp.abs(x)) / qmax, 1e-12)
            return jnp.clip(jnp.round(x / scale), -qmax - 1.0, qmax) * scale

        def fixed_qdq_u16(x):
            scale = 1.0 / 65536.0
            return jnp.clip(jnp.round(x / scale), 0.0, 65535.0) * scale

        def lpbq_dequant(w):
            O, I = w.shape
            qmax = 2.0 ** (W_BITS - 1) - 1.0
            wb = w.reshape(O, I // BLOCK, BLOCK)
            s = jnp.maximum(jnp.max(jnp.abs(wb), axis=-1, keepdims=True) / qmax, 1e-12)
            wq = jnp.clip(jnp.round(wb / s), -qmax - 1.0, qmax) * s
            return wq.reshape(O, I)
        x = act_qdq(x)
        up = act_qdq(x @ lpbq_dequant(w_up).T)
        gate = act_qdq(x @ lpbq_dequant(w_gate).T)
        sig = fixed_qdq_u16(jax.nn.sigmoid(gate))
        gate = act_qdq(gate * sig)
        o = act_qdq(gate * up)
        return o @ lpbq_dequant(w_down).T
    x = x + _L0_xattn_ref(_layernorm(x, axis=-1), ctx_1024, ctx_1024, L0_xattn_Wq, L0_xattn_bq, L0_xattn_Wk, L0_xattn_bk, L0_xattn_Wv, L0_xattn_bv, L0_xattn_Wo, L0_xattn_bo)
    x = x + _L0_ffn_ref(_layernorm(x, axis=-1), L0_ffn_w_gate, L0_ffn_w_up, L0_ffn_w_down)
    return x

_drawn_inputs = setup_inputs


def setup_inputs(seed=0):
    import zlib

    import numpy as np

    out = dict(_drawn_inputs(seed))
    spreads = {'L0_xattn_bq': (0.0, 0.433),
     'L0_xattn_bk': (0.0, 0.8),
     'L0_xattn_bv': (0.0, 0.1),
     'L0_xattn_bo': (0.0, 0.1)}
    factors = {}
    for name, (base, spread) in spreads.items():
        noise = np.random.default_rng([zlib.crc32(name.encode()), seed]).standard_normal(out[name].shape)
        drawn = base * np.exp(spread * noise) if base else spread * noise
        out[name] = jnp.asarray(drawn.astype(out[name].dtype))
    for name, factor in factors.items():
        out[name] = (out[name] * factor).astype(out[name].dtype)
    return out
```

```python
from contextlib import ExitStack, contextmanager

import concourse.bass as bass
from concourse import mybir

ALU = mybir.AluOpType
ACT = mybir.ActivationFunctionType
AX = mybir.AxisListType
F32 = mybir.dt.float32
F16 = mybir.dt.float16
BF16 = mybir.dt.bfloat16
I32 = mybir.dt.int32
I16 = mybir.dt.int16
U16 = mybir.dt.uint16
REDUCE = bass.bass_isa.ReduceOp

P = 128
BATCH, SEQ, D = 16, 256, 512
HEADS, HD = 16, 32
INNER = 1536
DC = D // P
TT = SEQ // P
IC = INNER // P
HG = P // HD
GROUPS = HEADS // HG
QBLOCK = 32
LN_EPS = 1e-5
STEP_FLOOR = 1e-12
TINY = 1e-30
EXPONENT = 0x7F800000
MAGIC = 1.5 * 2.0 ** 23
SCORE_SCALE = float(HD) ** -0.5
MASKED = -1e30
WMAX = 7.0
QMAX = 32767.0
SIG = 65536.0
HALF_TURN = [(k + HD // 2) % HD for k in range(HD)]
MATS = ("q", "k", "v", "o", "gate", "up", "down", "ctx")
MQ, MK, MV, MO, MG, MU, MD, MC = range(8)


class Tally:

    def __init__(self, start=0, by=1):
        self.value, self.by, self.made = start, by, 0

    def next(self):
        self.made += 1
        self.value = self.value + self.by
        return self.value


class Ring:

    def __init__(self, banks):
        self.banks, self.at = banks, 0
        self.fills = [Tally() for _ in range(banks)]

    def next(self):
        b = self.at % self.banks
        self.at += 1
        return b, self.fills[b].next()

    def back(self, k):
        b = (self.at - k) % self.banks
        return b, self.fills[b].value


@contextmanager
def loop(eng, lo, hi, tallies):
    start = [t.value for t, _ in tallies]
    with eng.Fori(lo, hi) as i:
        for (t, n), v in zip(tallies, start):
            t.value, t.made = v + (i - lo) * (t.by * n), 0
        yield i
        for k, (t, n) in enumerate(tallies):
            assert t.made == n, ("tally", k, "made", t.made, "said", n)
    for (t, n), v in zip(tallies, start):
        t.value = v + t.by * n * (hi - lo)


def row(view, i):
    if isinstance(i, int):
        return view[i]
    v = view[bass.ds(i, 1)]
    names = "abcd"[: len(v.shape) - 2]
    return v.rearrange(f"z p {' '.join(names)} -> (z p) {' '.join(names)}")


def split_scales(dve, link, dst_inv, dst_half, peak, power):
    link(dve.tensor_scalar(peak, peak, TINY, None, ALU.max))
    link(dve.tensor_scalar(power.bitcast(I32), peak.bitcast(I32), EXPONENT, None, ALU.bitwise_and))
    link(dve.tensor_scalar(dst_inv.bitcast(I32), power.bitcast(I32), EXPONENT, None, ALU.bitwise_xor))
    link(dve.tensor_scalar(dst_half, power, 0.5, None, ALU.mult))


def prepare(nc, io, keep):
    CH, RB = 4, 4
    n_ffn, n_ctx = 3 * IC // CH, BATCH * TT // CH
    n_peak = 4 + n_ffn + n_ctx
    with ExitStack() as ctx:
        def buf(name, shape, dt):
            return ctx.enter_context(nc.sbuf_tensor(name, shape, dt))

        def sem(name):
            return ctx.enter_context(nc.semaphore(name))

        raw_attn = buf("raw_attn", [P, 4 * CH, D], F32)
        raw = buf("raw", [P, RB, CH, D], F32)
        peak = buf("peak", [P, n_peak], F32)
        peak8 = buf("peak8", [P, 8], F32)
        top8 = buf("top8", [P, 8], F32)
        power8 = buf("power8", [P, 8], F32)
        wo32 = buf("wo32", [P, DC, D], F32)
        bv_cols = buf("bv_cols", [P, DC, P], F32)
        ones = buf("ones", [P, P], F32)
        w_raw = buf("w_raw", [P, 2, D], F32)
        w_deq = buf("w_deq", [P, 2, D], F32)
        block_max = buf("block_max", [P, D // QBLOCK], F32)
        step = buf("step", [P, D // QBLOCK], F32)
        per_step = buf("per_step", [P, D // QBLOCK], F32)
        parts = buf("parts", [P, 2, 2, DC, P], F16)
        banks = ctx.enter_context(nc.psum_tensor("prep_banks", [P, 4, D], F32))
        bias_bank = ctx.enter_context(nc.psum_tensor("bias_bank", [P, D], F32))

        attn_in = [sem(f"attn_in{k}") for k in range(4)]
        raw_in = [sem(f"raw_in{k}") for k in range(RB)]
        const_in = sem("const_in")
        peak_done = sem("peak_done")
        peaks_joined = sem("peaks_joined")
        top_ready = sem("top_ready")
        dve_step = sem("dve_step")
        scales_ready = sem("scales_ready")
        pool_step = sem("pool_step")
        ident_ready = sem("ident_ready")
        turned = sem("turned")
        hi_ready = sem("hi_ready")
        lo_ready = sem("lo_ready")
        wo_ready = sem("wo_ready")
        bv_ready = sem("bv_ready")
        bias_sum = sem("bias_sum")
        w_in = [sem(f"w_in{k}") for k in range(2)]
        w_quantised = sem("w_quantised")
        parts_stored = [sem(f"parts_stored{k}") for k in range(2)]
        block = ctx.enter_context(nc.Block())

        ffn_loads = io["ffn_w"].rearrange("(m u) p d -> m p u d", u=CH)
        attn_loads = io["attn_w"].rearrange("(m u) p d -> m p u d", u=CH)
        ctx_loads = io["ctx"].rearrange("b (t p) d -> p (b t) d", p=P)
        stores = io["w_parts"]

        @block.sync
        def _(sp):
            for k in range(4):
                sp.dma_start(raw_attn[:, k * CH:(k + 1) * CH, :], attn_loads[k]).then_inc(attn_in[k], 16)
            for name in ("cos", "sin", "bqk", "bv", "bias_row"):
                sp.dma_start(keep[name][:, :], io[name]).then_inc(const_in, 16)
            for k in range(n_ffn + n_ctx):
                if k >= RB:
                    sp.wait_ge(peak_done, 4 + k - RB + 1)
                src = ffn_loads[k] if k < n_ffn else ctx_loads[:, (k - n_ffn) * CH:(k - n_ffn + 1) * CH, :]
                sp.dma_start(raw[:, k % RB, :, :], src).then_inc(raw_in[k % RB], 16)
            quantised = Tally()
            lo = Tally(4 * DC)
            units = 3 * IC
            for b in range(2):
                sp.dma_start(w_raw[:, b, :], row(io["ffn_w"], b)).then_inc(w_in[b], 16)
            with loop(sp, 0, units // 2 - 1, [(quantised, 2), (lo, 2)]) as i:
                for b in range(2):
                    sp.wait_ge(w_quantised, quantised.next())
                    sp.dma_start(w_raw[:, b, :], row(io["ffn_w"], i * 2 + (2 + b))).then_inc(w_in[b], 16)
                for b in range(2):
                    sp.wait_ge(lo_ready, lo.next())
                    sp.dma_start(row(stores, i * 2 + b), parts[:, b]).then_inc(parts_stored[b], 16)
            for b in range(2):
                sp.wait_ge(lo_ready, lo.next())
                sp.dma_start(row(stores, units - 2 + b), parts[:, b]).then_inc(parts_stored[b], 16)
            for b in range(2):
                sp.wait_ge(parts_stored[b], 16 * (units // 2) + 16)

        @block.gpsimd
        def _(pool):
            pool.memset(keep["ident"][:, :], 0.0).then_inc(pool_step, 1)
            pool.memset(keep["ident_b"][:, :], 0.0).then_inc(pool_step, 1)
            pool.memset(keep["mask"][:, :], 0.0).then_inc(pool_step, 1)
            pool.memset(keep["minus_half"][:, :], -0.5).then_inc(pool_step, 1)
            pool.memset(ones[:, :], 1.0).then_inc(pool_step, 1)
            pool.wait_ge(pool_step, 5)
            for name in ("ident", "ident_b"):
                pool.affine_select(out=keep[name][:, :], in_=keep[name][:, :], compare_op=ALU.not_equal, fill=1.0,
                                   base=0, pattern=[[-1, P]], channel_multiplier=1).then_inc(ident_ready, 1)
            for at in (0, P):
                diag = keep["mask"][:, at:at + P]
                pool.affine_select(out=diag, in_=diag, compare_op=ALU.is_ge, fill=MASKED,
                                   base=0, pattern=[[-1, P]], channel_multiplier=1).then_inc(ident_ready, 1)
            pool.wait_ge(peaks_joined, 1)
            pool.partition_all_reduce(top8[:, :], peak8[:, :], P, REDUCE.max).then_inc(top_ready, 1)

        @block.vector
        def _(dve):
            done = Tally()

            def link(ins):
                ins.then_inc(dve_step, 1)
                dve.wait_ge(dve_step, done.next())

            fills = [0] * RB
            for k in range(n_peak):
                if k < 4:
                    dve.wait_ge(attn_in[k], 16)
                    src = raw_attn[:, k * CH:(k + 1) * CH, :]
                else:
                    b = (k - 4) % RB
                    fills[b] += 16
                    dve.wait_ge(raw_in[b], fills[b])
                    src = raw[:, b, :, :]
                dve.tensor_reduce(peak[:, k:k + 1], src, AX.XY, ALU.max, apply_absolute_value=True).then_inc(peak_done, 1)
            dve.wait_ge(peak_done, n_peak)
            dve.tensor_copy(peak8[:, 0:4], peak[:, 0:4]).then_inc(dve_step, 1)
            done.next()
            per = IC // CH
            dve.tensor_reduce(peak8[:, 4:7], peak[:, 4:4 + 3 * per].rearrange("p (m k) -> p m k", k=per), AX.X,
                              ALU.max).then_inc(dve_step, 1)
            done.next()
            link(dve.tensor_reduce(peak8[:, 7:8], peak[:, 4 + 3 * per:n_peak], AX.X, ALU.max))
            dve.tensor_copy(power8[:, :], peak8[:, :]).then_inc(peaks_joined, 1)
            dve.wait_ge(top_ready, 1)
            split_scales(dve, link, keep["inv"][:, :], keep["half"][:, :], top8[:, :], power8[:, :])
            half = keep["half"]
            link(dve.tensor_copy(keep["back"][:, 0:1], half[:, MQ:MQ + 1]))
            link(dve.tensor_tensor(keep["back"][:, 1:2], half[:, MK:MK + 1], half[:, MC:MC + 1], ALU.mult))
            link(dve.tensor_tensor(keep["back"][:, 2:3], half[:, MV:MV + 1], half[:, MC:MC + 1], ALU.mult))
            link(dve.tensor_tensor(keep["back"][:, 2:3], keep["back"][:, 2:3], half[:, MO:MO + 1], ALU.mult))
            link(dve.memset(keep["x2_peak"][:, :], 0.0))
            dve.wait_ge(ident_ready, 4)
            dve.wait_ge(const_in, 16 * 5)
            for c in range(DC):
                ins = dve.tensor_scalar(bv_cols[:, c, :], ones[:, :], keep["bv"][:, c:c + 1], None, ALU.mult)
                ins.then_inc(bv_ready, 1)
            dve.tensor_copy(power8[:, :], keep["inv"][:, :]).then_inc(scales_ready, 1)
            for u in range(4 * DC):
                dve.wait_ge(hi_ready, u + 1)
                m, r = u // DC, u % DC
                dve.scalar_tensor_tensor(
                    out=keep["attn_lo"][:, m, :, r * P:(r + 1) * P],
                    in0=banks[:, u % 4, :].rearrange("p (c o) -> p c o", c=DC), scalar=keep["inv"][:, m:m + 1],
                    in1=keep["attn_hi"][:, m, :, r * P:(r + 1) * P], op0=ALU.mult, op1=ALU.subtract).then_inc(lo_ready, 1)
            dve.wait_ge(bias_sum, 1)
            link(dve.tensor_tensor(keep["bias_row"][:, :], keep["bias_row"][:, :], bias_bank[:, :], ALU.add))

            hi = Tally(4 * DC)
            lo = Tally(4 * DC)
            loaded = [Tally(by=16) for _ in range(2)]
            stored = [Tally(by=16) for _ in range(2)]
            for m in (MG, MU, MD):
                inv = keep["inv"][:, m:m + 1]
                with loop(dve, 0, IC // 2, [(done, 14), (hi, 2), (lo, 2)] + [(t, 1) for t in loaded + stored]):
                    for b in range(2):
                        w = w_raw[:, b, :].rearrange("p (k j) -> p k j", j=QBLOCK)
                        q = w_deq[:, b, :].rearrange("p (k j) -> p k j", j=QBLOCK)
                        dve.wait_ge(w_in[b], loaded[b].next())
                        link(dve.tensor_reduce(block_max[:, :], w, AX.X, ALU.max, apply_absolute_value=True))
                        link(dve.tensor_scalar(step[:, :], block_max[:, :], 1.0 / WMAX, STEP_FLOOR, ALU.mult, ALU.max))
                        link(dve.reciprocal(per_step[:, :], step[:, :]))
                        link(dve.tensor_tensor(q, w, per_step[:, :].unsqueeze(2).to_broadcast([P, D // QBLOCK, QBLOCK]),
                                               ALU.mult))
                        link(dve.tensor_scalar(q, q, MAGIC, MAGIC + WMAX, ALU.add, ALU.min))
                        link(dve.tensor_scalar(q, q, MAGIC - WMAX - 1.0, MAGIC, ALU.max, ALU.subtract))
                        link(dve.tensor_scalar(step[:, :], step[:, :], inv, None, ALU.mult))
                        dve.tensor_tensor(q, q, step[:, :].unsqueeze(2).to_broadcast([P, D // QBLOCK, QBLOCK]),
                                          ALU.mult).then_inc(w_quantised, 1)
                    for b in range(2):
                        dve.wait_ge(hi_ready, hi.next())
                        dve.tensor_tensor(parts[:, b, 1].rearrange("p c o -> p (c o)"), banks[:, b, :],
                                          parts[:, b, 0].rearrange("p c o -> p (c o)"), ALU.subtract).then_inc(lo_ready, 1)
                        lo.next()
                        stored[b].next()

        @block.tensor
        def _(pe):
            pe.wait_ge(ident_ready, 2)
            for u in range(4 * DC):
                if u >= 4:
                    pe.wait_ge(lo_ready, u - 3)
                if u == 0:
                    for k in range(4):
                        pe.wait_ge(attn_in[k], 16)
                for c in range(DC):
                    last = pe.transpose(banks[:, u % 4, c * P:(c + 1) * P], raw_attn[:, u, c * P:(c + 1) * P],
                                        keep["ident"][:, :])
                last.then_inc(turned, 1)
            pe.wait_ge(wo_ready, DC)
            pe.wait_ge(bv_ready, DC)
            for c in range(DC):
                last = pe.matmul(bias_bank[:, :], bv_cols[:, c, :], wo32[:, c, :], start=(c == 0), stop=(c == DC - 1))
            last.then_inc(bias_sum, 1)
            quantised = Tally()
            lo = Tally(4 * DC - 2)
            with loop(pe, 0, 3 * IC // 2, [(quantised, 2), (lo, 2)]):
                for b in range(2):
                    pe.wait_ge(w_quantised, quantised.next())
                    pe.wait_ge(lo_ready, lo.next())
                    for c in range(DC):
                        last = pe.transpose(banks[:, b, c * P:(c + 1) * P], w_deq[:, b, c * P:(c + 1) * P],
                                            keep["ident"][:, :])
                    last.then_inc(turned, 1)

        @block.scalar
        def _(act):
            act.sem_inc(parts_stored[0], 16)
            act.sem_inc(parts_stored[1], 16)
            act.wait_ge(scales_ready, 1)
            for u in range(4 * DC):
                act.wait_ge(turned, u + 1)
                m, r = u // DC, u % DC
                src = banks[:, u % 4, :].rearrange("p (c o) -> p c o", c=DC)
                if m == MO:
                    act.activation(wo32[:, :, r * P:(r + 1) * P], src, ACT.Copy).then_inc(wo_ready, 1)
                act.activation(keep["attn_hi"][:, m, :, r * P:(r + 1) * P], src, ACT.Copy,
                               scale=keep["inv"][:, m:m + 1]).then_inc(hi_ready, 1)
            turn = Tally(4 * DC)
            stored = [Tally(by=16) for _ in range(2)]
            with loop(act, 0, 3 * IC // 2, [(turn, 2)] + [(t, 1) for t in stored]):
                for b in range(2):
                    act.wait_ge(turned, turn.next())
                    act.wait_ge(parts_stored[b], stored[b].next())
                    act.activation(parts[:, b, 0].rearrange("p c o -> p (c o)"), banks[:, b, :],
                                   ACT.Copy).then_inc(hi_ready, 1)


def turn_steps(i_in, nxt, nxt2, prev):
    steps = []
    for g in range(GROUPS):
        if i_in:
            steps.append(("scores", g))
        if g == 0:
            if prev:
                steps.append(("turn_p", GROUPS - 1))
            if i_in:
                steps.append(("value", 0))
            if prev:
                steps.append(("apply", GROUPS - 1))
            if nxt:
                steps.append(("turn", 0))
            if prev:
                steps.append(("out", 0))
            if nxt:
                steps.append(("query_key", 0))
        else:
            if i_in:
                steps.append(("turn_p", g - 1))
            if nxt:
                steps.append(("query_key", g))
            if i_in:
                steps.append(("apply", g - 1))
        if g == 1 and i_in:
            steps.append(("residual", 0))
        if g == 2 and prev:
            steps.append(("turn_x2", 0))
        if g == 2 and nxt2:
            steps.append(("norm", 0))
    return steps


def turns(eng, turn, tallies):
    turn(-2, turn_steps(False, False, True, False), 0)
    turn(-1, turn_steps(False, True, True, False), 1)
    turn(0, turn_steps(True, True, True, False), 0)
    middle = turn_steps(True, True, True, True)
    with loop(eng, 0, (BATCH - 4) // 2, [(t, 2 * n // over) for t, n, over in tallies]) as k:
        for half in range(2):
            turn(k * 2 + (1 + half), middle, 1 - half)
    turn(BATCH - 3, middle, 1)
    turn(BATCH - 2, turn_steps(True, True, False, True), 0)
    turn(BATCH - 1, turn_steps(True, False, False, True), 1)
    turn(BATCH, turn_steps(False, False, False, True), 0)


def attend(nc, io, keep):
    RING = 4
    FILLS = 4 * GROUPS + TT + 2 * TT + TT + GROUPS + TT
    with ExitStack() as ctx:
        def buf(name, shape, dt):
            return ctx.enter_context(nc.sbuf_tensor(name, shape, dt))

        def sem(name):
            return ctx.enter_context(nc.semaphore(name))

        x_in = buf("x_in", [P, TT, D], F32)
        c_in = buf("c_in", [P, TT, D], F32)
        x_res = buf("x_res", [P, TT, D], F32)
        xb = buf("xb", [P, TT, D], F32)
        stats = buf("stats", [P, TT, 6], F32)
        mean = buf("mean", [P, TT], F32)
        half_gap = buf("half_gap", [P, TT], F32)
        spread = buf("spread", [P, TT], F32)
        var_eps = buf("var_eps", [P, TT], F32)
        rstd = buf("rstd", [P, TT], F32)
        xn = buf("xn", [P, TT, D], F32)
        xt = buf("xt", [P, 2, DC, SEQ], F16)
        ct = buf("ct", [P, 2, DC, SEQ], F16)
        raw = buf("raw_qk", [P, 2, 2, SEQ], F32)
        by_sin = buf("by_sin", [P, 2, SEQ], F32)
        by_cos = buf("by_cos", [P, 2, SEQ], F32)
        sin_turned = buf("sin_turned", [P, 2, SEQ], F32)
        qk = buf("qk", [P, GROUPS, 2, SEQ], F32)
        v = buf("v", [P, 2, TT, D], F32)
        neg_max = buf("neg_max", [P, 2, HG], F32)
        prob = buf("prob", [P, 2, HG, 3 * P], F32)
        row_sum = buf("row_sum", [P, 2, 2, HG], F32)
        per_sum = buf("per_sum", [P, 2, 2, HG], F32)
        pt0 = buf("pt0", [P, HG, SEQ], F32)
        pt1 = buf("pt1", [P, HG, P], F32)
        ot = buf("ot", [P, 2, GROUPS, SEQ], F16)
        x2 = buf("x2", [P, TT, D], F32)
        stats2 = buf("stats2", [P, TT, 6], F32)
        mean2 = buf("mean2", [P, TT], F32)
        var_eps2 = buf("var_eps2", [P, TT], F32)
        rstd2 = buf("rstd2", [P, TT], F32)
        xn2 = buf("xn2", [P, TT, D], F32)
        xn2_peak = buf("xn2_peak", [P, 1], F32)
        xt2 = buf("xt2", [P, DC, SEQ], F32)
        score_banks = ctx.enter_context(nc.psum_tensor("score_banks", [P, HG, D], F32))
        banks = ctx.enter_context(nc.psum_tensor("ring_banks", [P, RING, D], F32))

        x_loaded, c_loaded, res_loaded = sem("x_loaded"), sem("c_loaded"), sem("res_loaded")
        x2_stored, xt2_stored = sem("x2_stored"), sem("xt2_stored")
        var_ready, rstd_ready = sem("var_ready"), sem("rstd_ready")
        var2_ready, rstd2_ready = sem("var2_ready"), sem("rstd2_ready")
        xn_ready = sem("xn_ready")
        xb_ready, x2_ready, xn2_ready = sem("xb_ready"), sem("x2_ready"), sem("xn2_ready")
        filled = [sem(f"filled{b}") for b in range(RING)]
        emptied = [sem(f"emptied{b}") for b in range(RING)]
        turn_hi, heads_hi = sem("turn_hi"), sem("heads_hi")
        raw_used, rotated = sem("raw_used"), sem("rotated")
        scored, max_ready, exped, sums_ready = sem("scored"), sem("max_ready"), sem("exped"), sem("sums_ready")
        normed = sem("normed")
        dve_step = sem("attn_dve_step")
        block = ctx.enter_context(nc.Block())

        x_tiles = io["x"].rearrange("b (t p) d -> b p t d", p=P)
        c_tiles = io["ctx"].rearrange("b (t p) d -> b p t d", p=P)
        x2_tiles = io["x2"].rearrange("b (t p) d -> b p t d", p=P)

        @block.sync
        def _(sp):
            def turn(i, steps, par):
                names = [s for s, _ in steps]
                if "norm" in names:
                    if not isinstance(i, int) or i + 2 > 0:
                        sp.wait_ge(xn_ready, i + 2)
                    sp.dma_start(x_in[:, :, :], row(x_tiles, i + 2)).then_inc(x_loaded, 16)
                if "residual" in names:
                    if not isinstance(i, int) or i > 0:
                        sp.wait_ge(xb_ready, i)
                    sp.dma_start(x_res[:, :, :], row(x_tiles, i)).then_inc(res_loaded, 16)
                if "norm" in names:
                    if not isinstance(i, int) or i + 2 > 0:
                        sp.wait_ge(turn_hi, i * (2 * TT) + 4 * TT)
                    sp.dma_start(c_in[:, :, :], row(c_tiles, i + 2)).then_inc(c_loaded, 16)
                if "out" in names:
                    sp.wait_ge(x2_ready, TT * i)
                    sp.dma_start(row(x2_tiles, i - 1), x2[:, :, :]).then_inc(x2_stored, 16)
                    b, n = ring_job(steps)
                    sp.wait_ge(emptied[b], n + 1)
                    sp.dma_start(row(io["xt2"], i - 1), xt2[:, :, :]).then_inc(xt2_stored, 16)
                else:
                    ring_job(steps)

            ring = Ring(RING)

            def ring_job(steps):
                count = {"turn_p": 3, "apply": 1, "value": TT, "turn": 2 * TT, "out": TT, "query_key": 1, "turn_x2": TT}
                mine = None
                for s, _ in steps:
                    for _ in range(count.get(s, 0)):
                        last = ring.next()
                    if s == "turn_x2":
                        mine = last
                return mine

            turns(sp, turn, [(f, FILLS, RING) for f in ring.fills])
            sp.wait_ge(x2_stored, 16 * BATCH)
            sp.wait_ge(xt2_stored, 16 * BATCH)

        @block.gpsimd
        def _(pool):
            def turn(i, steps, par):
                for s, g in steps:
                    if s == "norm":
                        pool.wait_ge(var_ready, i + 3)
                        pool.tensor_tensor(rstd[:, :], var_eps[:, :], keep["minus_half"][:, :],
                                           ALU.pow).then_inc(rstd_ready, 1)
                    if s == "out":
                        pool.wait_ge(var2_ready, i)
                        pool.tensor_tensor(rstd2[:, :], var_eps2[:, :], keep["minus_half"][:, :],
                                           ALU.pow).then_inc(rstd2_ready, 1)
                    if s == "residual":
                        pool.wait_ge(res_loaded, i * 16 + 16)
                        if not isinstance(i, int) or i > 0:
                            pool.wait_ge(x2_ready, i * TT)
                        pool.tensor_tensor(xb[:, :, :], x_res[:, :, :],
                                           keep["bias_row"][:, :].unsqueeze(1).to_broadcast([P, TT, D]),
                                           ALU.add).then_inc(xb_ready, 1)
                    if s == "scores":
                        pool.wait_ge(sums_ready, i * GROUPS + (g + 1))
                        pr, ps = prob[:, g % 2], per_sum[:, g % 2]
                        pool.tensor_tensor(pr[:, :, 0:P], pr[:, :, 0:P],
                                           ps[:, 0, :].unsqueeze(2).to_broadcast([P, HG, P]), ALU.mult)
                        pool.tensor_tensor(pr[:, :, P:3 * P], pr[:, :, P:3 * P],
                                           ps[:, 1, :].unsqueeze(2).to_broadcast([P, HG, 2 * P]),
                                           ALU.mult).then_inc(normed, 1)

            turns(pool, turn, [])

        @block.vector
        def _(dve):
            ring = Ring(RING)
            done = Tally()

            def link(ins):
                ins.then_inc(dve_step, 1)
                dve.wait_ge(dve_step, done.next())

            def mean_and_var(st, mean, var_eps):
                dve.tensor_tensor(mean[:, :], st[:, :, 1], st[:, :, 4], ALU.add).then_inc(dve_step, 1)
                done.next()
                dve.tensor_tensor(half_gap[:, :], st[:, :, 1], st[:, :, 4], ALU.subtract).then_inc(dve_step, 1)
                done.next()
                link(dve.tensor_tensor(spread[:, :], st[:, :, 2], st[:, :, 5], ALU.add))
                dve.tensor_scalar(mean[:, :], mean[:, :], 0.5, None, ALU.mult).then_inc(dve_step, 1)
                done.next()
                link(dve.tensor_scalar(half_gap[:, :], half_gap[:, :], 0.5, None, ALU.mult))
                dve.tensor_scalar(spread[:, :], spread[:, :], 1.0 / D, LN_EPS, ALU.mult, ALU.add).then_inc(dve_step, 1)
                done.next()
                link(dve.tensor_tensor(half_gap[:, :], half_gap[:, :], half_gap[:, :], ALU.mult))
                return dve.tensor_tensor(var_eps[:, :], spread[:, :], half_gap[:, :], ALU.add)

            def per_row_sum(i, g):
                dve.wait_ge(exped, i * GROUPS + (g + 1))
                dve.reciprocal(per_sum[:, g % 2], row_sum[:, g % 2]).then_inc(sums_ready, 1)

            def rotate(g, b, n):
                src = raw[:, g % 2]
                sin = keep["sin"][:, :].unsqueeze(1).to_broadcast([P, 2, SEQ])
                cos = keep["cos"][:, :].unsqueeze(1).to_broadcast([P, 2, SEQ])
                dve.wait_ge(emptied[b], n + 1)
                link(dve.tensor_tensor(by_sin[:, :, :], src, sin, ALU.mult))
                dve.tensor_tensor(by_cos[:, :, :], src, cos, ALU.mult).then_inc(raw_used, 1)
                dve.stream_shuffle(sin_turned[:, :, :].rearrange("p a t -> p (a t)"),
                                   by_sin[:, :, :].rearrange("p a t -> p (a t)"), HALF_TURN).then_inc(dve_step, 1)
                dve.wait_ge(dve_step, done.next())
                dve.tensor_tensor(qk[:, g], by_cos[:, :, :], sin_turned[:, :, :], ALU.add).then_inc(rotated, 1)

            def turn(i, steps, par):
                names = [s for s, _ in steps]
                late = []
                if "scores" in names and "out" in names:
                    late.append((rotate, (GROUPS - 1, *ring.back(2))))
                waiting = False
                for s, g in steps:
                    if waiting and s != "turn_p":
                        for f, args in late:
                            f(*args)
                        late, waiting = [], False
                    if s == "norm":
                        dve.wait_ge(x_loaded, i * 16 + 48)
                        for t in range(TT):
                            ins = dve.bn_stats(stats[:, t, :], x_in[:, t, :])
                            if t == TT - 1:
                                link(ins)
                        mean_and_var(stats, mean, var_eps).then_inc(var_ready, 1)
                        dve.wait_ge(rstd_ready, i + 3)
                        for t in range(TT):
                            last = dve.tensor_scalar(xn[:, t, :], x_in[:, t, :], mean[:, t:t + 1], rstd[:, t:t + 1],
                                                     ALU.subtract, ALU.mult)
                        last.then_inc(xn_ready, 1)
                    if s == "turn":
                        for k in range(2 * TT):
                            b, n = ring.next()
                            dve.wait_ge(turn_hi, i * (2 * TT) + (2 * TT + k + 1))
                            t = k % TT
                            src = banks[:, b, :].rearrange("p (c o) -> p c o", c=DC)
                            if k < TT:
                                dve.tensor_tensor(xt[:, 1, :, t * P:(t + 1) * P], src, xt[:, 0, :, t * P:(t + 1) * P],
                                                  ALU.subtract).then_inc(emptied[b], 1)
                            else:
                                dve.scalar_tensor_tensor(
                                    out=ct[:, 1, :, t * P:(t + 1) * P], in0=src, scalar=keep["inv"][:, MC:MC + 1],
                                    in1=ct[:, 0, :, t * P:(t + 1) * P], op0=ALU.mult,
                                    op1=ALU.subtract).then_inc(emptied[b], 1)
                    if s == "value":
                        for _ in range(TT):
                            ring.next()
                    if s == "query_key":
                        b, n = ring.next()
                        if "scores" in names:
                            late.append((rotate, (g, b, n)))
                        else:
                            rotate(g, b, n)
                    if s == "scores":
                        dve.wait_ge(scored, i * GROUPS + (g + 1))
                        dve.tensor_reduce(neg_max[:, 0, :], score_banks[:, :, 0:P], AX.X, ALU.max,
                                          negate=True).then_inc(dve_step, 1)
                        done.next()
                        link(dve.tensor_reduce(neg_max[:, 1, :], score_banks[:, :, P:3 * P], AX.X, ALU.max, negate=True))
                        dve.tensor_scalar(neg_max[:, :, :], neg_max[:, :, :], SCORE_SCALE, None,
                                          ALU.mult).then_inc(max_ready, 1)
                        late.append((per_row_sum, (i, g)))
                        waiting = True
                    if s == "turn_p":
                        ring.next(), ring.next()
                        b, n = ring.next()
                        dve.wait_ge(filled[b], n)
                        dve.tensor_copy(pt1[:, :, :], banks[:, b, :].rearrange("p (h q) -> p h q", h=HG)).then_inc(emptied[b], 1)
                    if s == "apply":
                        ib = i - 1 if g == GROUPS - 1 else i
                        b, n = ring.next()
                        dve.wait_ge(heads_hi, ib * GROUPS + (g + 1))
                        dve.tensor_tensor(ot[:, 1, g, :], banks[:, b, 0:SEQ], ot[:, 0, g, :],
                                          ALU.subtract).then_inc(emptied[b], 1)
                    if s == "out":
                        if not isinstance(i, int) or i > 1:
                            dve.wait_ge(x2_stored, i * 16 - 16)
                        dve.wait_ge(xb_ready, i)
                        for t in range(TT):
                            b, n = ring.next()
                            dve.wait_ge(filled[b], n)
                            dve.scalar_tensor_tensor(out=x2[:, t, :], in0=banks[:, b, :], scalar=keep["back"][:, 2:3],
                                                     in1=xb[:, t, :], op0=ALU.mult, op1=ALU.add).then_inc(emptied[b], 1)
                            dve.wait_ge(emptied[b], n + 1)
                            dve.bn_stats(stats2[:, t, :], x2[:, t, :]).then_inc(x2_ready, 1)
                        dve.wait_ge(x2_ready, i * TT)
                        mean_and_var(stats2, mean2, var_eps2).then_inc(var2_ready, 1)
                        dve.wait_ge(rstd2_ready, i)
                        for t in range(TT):
                            last = dve.tensor_scalar(xn2[:, t, :], x2[:, t, :], mean2[:, t:t + 1], rstd2[:, t:t + 1],
                                                     ALU.subtract, ALU.mult)
                        last.then_inc(xn2_ready, 1)
                        dve.wait_ge(xn2_ready, i)
                        link(dve.tensor_reduce(xn2_peak[:, :], xn2[:, :, :], AX.XY, ALU.max, apply_absolute_value=True))
                        link(dve.tensor_tensor(keep["x2_peak"][:, :], keep["x2_peak"][:, :], xn2_peak[:, :], ALU.max))
                    if s == "turn_x2":
                        for _ in range(TT):
                            ring.next()

            links = 1 + 7 + GROUPS * 2 + GROUPS * 2 + 7 + 2
            turns(dve, turn, [(f, FILLS, RING) for f in ring.fills] + [(done, links, 1)])

        @block.scalar
        def _(act):
            ring = Ring(RING)
            for b in range(RING):
                act.sem_inc(emptied[b], 1)
            act.sem_inc(raw_used, 2)

            def exps(i, g):
                act.wait_ge(max_ready, i * GROUPS + (g + 1))
                for h in range(HG):
                    for part, (lo, hi) in enumerate(((0, P), (P, 3 * P))):
                        last = act.activation(prob[:, g % 2, h, lo:hi], score_banks[:, h, lo:hi], ACT.Exp,
                                              bias=neg_max[:, part, h:h + 1], scale=SCORE_SCALE,
                                              accum_out=row_sum[:, g % 2, part, h:h + 1])
                last.then_inc(exped, 1)

            def turn(i, steps, par):
                pending = None
                for s, g in steps:
                    if pending is not None and s != "turn_p":
                        exps(*pending)
                        pending = None
                    if s == "turn":
                        for k in range(2 * TT):
                            b, n = ring.next()
                            t = k % TT
                            src = banks[:, b, :].rearrange("p (c o) -> p c o", c=DC)
                            act.wait_ge(filled[b], n)
                            if k < TT:
                                act.activation(xt[:, 0, :, t * P:(t + 1) * P], src, ACT.Copy).then_inc(turn_hi, 1)
                            else:
                                act.activation(ct[:, 0, :, t * P:(t + 1) * P], src, ACT.Copy,
                                               scale=keep["inv"][:, MC:MC + 1]).then_inc(turn_hi, 1)
                    if s == "value":
                        for t in range(TT):
                            b, n = ring.next()
                            act.wait_ge(filled[b], n)
                            act.activation(v[:, par, t, :], banks[:, b, :], ACT.Copy).then_inc(emptied[b], 1)
                    if s == "query_key":
                        b, n = ring.next()
                        act.wait_ge(filled[b], n)
                        act.wait_ge(raw_used, i * GROUPS + (GROUPS + g + 1))
                        act.activation(raw[:, g % 2, 0, :], banks[:, b, 0:SEQ], ACT.Identity,
                                       bias=keep["bqk"][:, g:g + 1], scale=keep["back"][:, 0:1])
                        act.activation(raw[:, g % 2, 1, :], banks[:, b, SEQ:2 * SEQ], ACT.Identity,
                                       bias=keep["bqk"][:, DC + g:DC + g + 1],
                                       scale=keep["back"][:, 1:2]).then_inc(emptied[b], 1)
                    if s == "scores":
                        pending = (i, g)
                    if s == "turn_p":
                        for half in range(2):
                            b, n = ring.next()
                            act.wait_ge(filled[b], n)
                            act.activation(pt0[:, 2 * half:2 * half + 2, :],
                                           banks[:, b, :].rearrange("p (h q) -> p h q", h=2),
                                           ACT.Copy).then_inc(emptied[b], 1)
                        ring.next()
                        if pending is not None:
                            exps(*pending)
                            pending = None
                    if s == "apply":
                        b, n = ring.next()
                        act.wait_ge(filled[b], n)
                        act.activation(ot[:, 0, g, :], banks[:, b, 0:SEQ], ACT.Copy).then_inc(heads_hi, 1)
                    if s == "out":
                        for _ in range(TT):
                            ring.next()
                    if s == "turn_x2":
                        if not isinstance(i, int) or i > 1:
                            act.wait_ge(xt2_stored, i * 16 - 16)
                        for t in range(TT):
                            b, n = ring.next()
                            act.wait_ge(filled[b], n)
                            act.activation(xt2[:, :, t * P:(t + 1) * P],
                                           banks[:, b, :].rearrange("p (c o) -> p c o", c=DC),
                                           ACT.Copy).then_inc(emptied[b], 1)
                if pending is not None:
                    exps(*pending)

            turns(act, turn, [(f, FILLS, RING) for f in ring.fills])

        @block.tensor
        def _(pe):
            ring = Ring(RING)
            attn_hi, attn_lo, ident = keep["attn_hi"], keep["attn_lo"], keep["ident"]

            def fill():
                b, n = ring.next()
                pe.wait_ge(emptied[b], n)
                return b, n

            def three(out, pairs):
                count = 3 * len(pairs)
                k = 0
                for (w_hi, w_lo), (m_hi, m_lo) in pairs:
                    for w, m in ((w_hi, m_hi), (w_hi, m_lo), (w_lo, m_hi)):
                        last = pe.matmul(out, w, m, start=(k == 0), stop=(k == count - 1))
                        k += 1
                return last

            def turn(i, steps, par):
                for s, g in steps:
                    if s == "turn":
                        for k in range(2 * TT):
                            b, n = fill()
                            if k == 0:
                                pe.wait_ge(xn_ready, i + 2)
                            if k == TT:
                                pe.wait_ge(c_loaded, i * 16 + 32)
                            src = xn if k < TT else c_in
                            for c in range(DC):
                                last = pe.transpose(banks[:, b, c * P:(c + 1) * P], src[:, k % TT, c * P:(c + 1) * P],
                                                    ident[:, :])
                            last.then_inc(filled[b], 1)
                            turned = (b, n + 1)
                    if s == "value":
                        for t in range(TT):
                            b, n = fill()
                            tile = slice(t * P, (t + 1) * P)
                            three(banks[:, b, :], [((ct[:, 0, c, tile], ct[:, 1, c, tile]),
                                                    (attn_hi[:, MV, c, :], attn_lo[:, MV, c, :]))
                                                   for c in range(DC)]).then_inc(filled[b], 1)
                            v_out = (b, n + 1)
                    if s == "query_key":
                        if g == 0:
                            pe.wait_ge(emptied[turned[0]], turned[1])
                        b, n = fill()
                        cols = slice(g * P, (g + 1) * P)
                        for m, src in ((MQ, xt), (MK, ct)):
                            last = three(banks[:, b, m * SEQ:(m + 1) * SEQ],
                                         [((attn_hi[:, m, c, cols], attn_lo[:, m, c, cols]),
                                           (src[:, 0, c, :], src[:, 1, c, :])) for c in range(DC)])
                        last.then_inc(filled[b], 1)
                    if s == "scores":
                        pe.wait_ge(rotated, i * GROUPS + (g + 1))
                        if g > 0 or not isinstance(i, int) or i > 0:
                            pe.wait_ge(exped, i * GROUPS + g)
                        for h in range(HG):
                            f = slice(h * HD, (h + 1) * HD)
                            pe.matmul(score_banks[:, h, 0:P], qk[f, g, 0, 0:P], qk[f, g, 1, 0:P], start=True, stop=False)
                        for h in range(HG):
                            f = slice(h * HD, (h + 1) * HD)
                            pe.matmul(score_banks[:, h, P:3 * P], qk[f, g, 0, P:2 * P], qk[f, g, 1, :],
                                      start=False, stop=False)
                        for h in range(HG):
                            last = pe.matmul(score_banks[:, h, :].rearrange("p (a c) -> p a c", c=2 * P)[:, :, 0:P],
                                             keep["ident_b"][:, :], keep["mask"][:, :], start=False, stop=True)
                        last.then_inc(scored, 1)
                    if s == "turn_p":
                        ib = i - 1 if g == GROUPS - 1 else i
                        pe.wait_ge(normed, ib * GROUPS + (g + 1))
                        outs = []
                        for half in range(2):
                            b, n = fill()
                            for h in range(2):
                                for q in range(TT):
                                    last = pe.transpose(banks[:, b, h * SEQ + q * P:h * SEQ + (q + 1) * P],
                                                        prob[:, g % 2, 2 * half + h, q * P:(q + 1) * P], ident[:, :])
                            last.then_inc(filled[b], 1)
                            outs.append((b, n + 1))
                        b, n = fill()
                        for h in range(HG):
                            last = pe.transpose(banks[:, b, h * P:(h + 1) * P], prob[:, g % 2, h, 2 * P:3 * P], ident[:, :])
                        last.then_inc(filled[b], 1)
                        outs.append((b, n + 1))
                    if s == "apply":
                        vp = v[:, 1 - par if g == GROUPS - 1 else par]
                        b, n = fill()
                        for k, n_out in outs:
                            pe.wait_ge(emptied[k], n_out)
                        for h in range(HG):
                            cols = slice((g * HG + h) * HD, (g * HG + h + 1) * HD)
                            pe.matmul(banks[h * HD:(h + 1) * HD, b, 0:SEQ], vp[:, 0, cols], pt0[:, h, :],
                                      start=True, stop=False)
                        for h in range(HG):
                            cols = slice((g * HG + h) * HD, (g * HG + h + 1) * HD)
                            last = pe.matmul(banks[h * HD:(h + 1) * HD, b, P:SEQ], vp[:, 1, cols], pt1[:, h, :],
                                             start=False, stop=True)
                        last.then_inc(filled[b], 1)
                        heads_out = (b, n + 1)
                    if s == "out":
                        pe.wait_ge(emptied[heads_out[0]], heads_out[1])
                        for t in range(TT):
                            b, n = fill()
                            tile = slice(t * P, (t + 1) * P)
                            three(banks[:, b, :], [((ot[:, 0, c, tile], ot[:, 1, c, tile]),
                                                    (attn_hi[:, MO, c, :], attn_lo[:, MO, c, :]))
                                                   for c in range(DC)]).then_inc(filled[b], 1)
                    if s == "turn_x2":
                        pe.wait_ge(xn2_ready, i)
                        for t in range(TT):
                            b, n = fill()
                            for c in range(DC):
                                last = pe.transpose(banks[:, b, c * P:(c + 1) * P], xn2[:, t, c * P:(c + 1) * P], ident[:, :])
                            last.then_inc(filled[b], 1)

            turns(pe, turn, [(f, FILLS, RING) for f in ring.fills])


N = 512
TOK = BATCH * SEQ
NG = TOK // N
W2 = 2 * N
PIECES = TOK // W2


def hold(eng, sem, value, held):
    eng.wait_ge(sem, value)
    eng.sem_inc(held, 1)


class Scales:
    names = ("top", "x_step", "x_per", "g_step", "g_per", "a_step", "a_per", "a_unit", "a_fold",
             "u_step", "u_per", "o_step", "o_per", "o_unit", "o_fold", "g_back", "u_back", "d_back")

    def __init__(self, tile):
        self.tile = tile

    def __getitem__(self, name):
        k = self.names.index(name)
        return self.tile[:, k:k + 1]


def quantum(dve, link, sc, what, unit=None):
    if unit is not None:
        link(dve.tensor_tensor(sc["top"], sc["top"], unit, ALU.mult))
    link(dve.tensor_scalar(sc[what + "_step"], sc["top"], 1.0 / QMAX, STEP_FLOOR, ALU.mult, ALU.max))
    link(dve.reciprocal(sc[what + "_per"], sc[what + "_step"]))


def project(nc, io, keep, sc, xq, qg, phase):
    up = phase == "up"
    turns_of_2 = IC // 2
    with ExitStack() as ctx:
        def buf(name, shape, dt):
            return ctx.enter_context(nc.sbuf_tensor(f"{phase}_{name}", shape, dt))

        def sem(name):
            return ctx.enter_context(nc.semaphore(f"{phase}_{name}"))

        ST, CB = 2, 4
        w = buf("w", [P, 2, 2, DC, P], F16)
        stage = buf("stage", [P, ST, W2], F32)
        peaks = buf("peaks", [P, 2 * PIECES], F32)
        if up:
            chain = buf("chain", [P, CB, W2], F32)
            sig_steps = buf("sig_steps", [P, W2], U16)
            act_peaks = buf("act_peaks", [P, 4 * PIECES], F32)
        else:
            xt_in = buf("xt_in", [P, 2, DC, N], F32)
            x_steps = buf("x_steps", [P, DC, N], I16)
        banks = ctx.enter_context(nc.psum_tensor(f"{phase}_banks", [P, 4, 2, N], F32))

        w_in = [sem(f"w_in{b}") for b in range(2)]
        xt_loaded = [sem(f"xt_loaded{b}") for b in range(2)]
        xq_ready = sem("xq_ready")
        filled, staged, peaked = sem("filled"), sem("staged"), sem("peaked")
        stored = [sem(f"stored{b}") for b in range(ST)]
        joined, top_ready, scales_ready = sem("joined"), sem("top_ready"), sem("scales_ready")
        joined2, top2_ready, scales2_ready = sem("joined2"), sem("top2_ready"), sem("scales2_ready")
        chain_in = [sem(f"chain_in{b}") for b in range(CB)]
        steps_ready, sig_ready, act_done, act_steps = sem("steps_ready"), sem("sig_ready"), sem("act_done"), sem("act_steps")
        dve_step, held_act = sem("dve_step"), sem("held_act")
        block = ctx.enter_context(nc.Block())

        dst = (io["ups"] if up else io["gates"]).rearrange("m p (j c) -> m p j c", c=W2)
        gates = io["gates"].rearrange("(k a) p (j c) -> k p a j c", c=W2, a=4)
        w_units = io["w_parts"][IC:2 * IC] if up else io["w_parts"][0:IC]
        run_peak = keep["run_peak"]
        act_run = keep["act_peak"]

        @block.sync
        def _(sp):
            for b in range(2):
                sp.dma_start(w[:, b], w_units[b]).then_inc(w_in[b], 16)
            if not up:
                for n in range(NG):
                    if n >= 2:
                        sp.wait_ge(xq_ready, n - 1)
                    for j in range(N // SEQ):
                        sp.dma_start(xt_in[:, n % 2, :, j * SEQ:(j + 1) * SEQ],
                                     io["xt2"][n * (N // SEQ) + j]).then_inc(xt_loaded[n % 2], 16)
            piece, used = Tally(), [Tally(), Tally()]
            fills = Tally()

            def store_all(i):
                for a in range(2):
                    for j in range(PIECES):
                        sp.wait_ge(staged, piece.next())
                        sp.dma_start(row(dst, i * 2 + a)[:, j, :], stage[:, j % ST, :]).then_inc(stored[j % ST], 16)

            def weights(i, b):
                sp.wait_ge(filled, fills.value)
                sp.dma_start(w[:, b], row(w_units, i * 2 + (2 + b))).then_inc(w_in[b], 16)

            acts = Tally()
            n_chain = 4 * PIECES

            def turn(i, second, more, chain_first):
                c = 0
                for a in range(2):
                    for j in range(PIECES):
                        if up and not second:
                            for _ in range(2):
                                if chain_first and c < CB:
                                    pass
                                else:
                                    sp.wait_ge(act_done, acts.next())
                                q, r = divmod(c, PIECES)
                                g = row(gates, i)[:, q, r, :]
                                sp.dma_start(chain[:, c % CB, :], g).then_inc(chain_in[c % CB], 16)
                                c += 1
                        sp.wait_ge(staged, piece.next())
                        sp.dma_start(row(dst, i * 2 + a)[:, j, :], stage[:, j % ST, :]).then_inc(stored[j % ST], 16)
                    fills.value = fills.value + PIECES
                    fills.made += 1
                    if more:
                        weights(i, a)

            third = turns_of_2 // 2
            if up:
                turn(0, False, True, True)
                with loop(sp, 1, third, [(piece, 2 * PIECES), (acts, n_chain)]) as i:
                    fills.value = i * (2 * PIECES)
                    turn(i, False, True, False)
                with loop(sp, third, turns_of_2 - 1, [(piece, 2 * PIECES)]) as i:
                    fills.value = i * (2 * PIECES)
                    turn(i, True, True, False)
            else:
                with loop(sp, 0, turns_of_2 - 1, [(piece, 2 * PIECES)]) as i:
                    fills.value = i * (2 * PIECES)
                    turn(i, True, True, False)
            turn(turns_of_2 - 1, True, False, False)
            for b in range(ST):
                sp.wait_ge(stored[b], 16 * (IC * PIECES // ST + 1))

        @block.tensor
        def _(pe):
            weights_in = [Tally(by=16), Tally(by=16)]
            emptied = Tally(-4)

            def turn(i, first):
                for a in range(2):
                    pe.wait_ge(w_in[a], weights_in[a].next())
                    for j in range(PIECES):
                        if first and a == 0:
                            if not up:
                                pe.wait_ge(xq_ready, 2 * j + 1)
                            emptied.next()
                        else:
                            pe.wait_ge(staged, emptied.next())
                        for half in range(2):
                            n = 2 * j + half
                            if first and a == 0 and half and not up:
                                pe.wait_ge(xq_ready, n + 1)
                            k = 0
                            for c in range(DC):
                                for wp, xp in ((0, 0), (0, 1), (1, 0)):
                                    last = pe.matmul(banks[:, j, half, :], w[:, a, wp, c, :], xq[:, xp, n, c, :],
                                                     start=(k == 0), stop=(k == 3 * DC - 1))
                                    k += 1
                        last.then_inc(filled, 1)

            turn(0, True)
            with loop(pe, 1, turns_of_2, [(weights_in[0], 1), (weights_in[1], 1), (emptied, 2 * PIECES)]) as i:
                turn(i, False)

        @block.scalar
        def _(act):
            for b in range(ST):
                act.sem_inc(stored[b], 16)
            act.sem_inc(peaked, ST)
            back = sc["u_back"] if up else sc["g_back"]
            fills, free = Tally(), Tally()
            store = [Tally(by=16) for _ in range(ST)]
            act.wait_ge(scales_ready, 1)

            def evacuate(j):
                act.wait_ge(filled, fills.next())
                act.wait_ge(peaked, free.next())
                act.wait_ge(stored[j % ST], store[j % ST].next())
                act.activation(stage[:, j % ST, :], banks[:, j].rearrange("p h n -> p (h n)"), ACT.Copy,
                               scale=back).then_inc(staged, 1)

            per_turn = [(fills, 2 * PIECES), (free, 2 * PIECES)] + [(t, 2 * PIECES // ST) for t in store]
            if not up:
                with loop(act, 0, turns_of_2, per_turn):
                    for a in range(2):
                        for j in range(PIECES):
                            evacuate(j)
                return

            loads = [Tally(by=16) for _ in range(CB)]
            steps, sigs, acts = Tally(), Tally(), Tally()

            def piece_of(k, c):
                q, r = divmod(c, PIECES)
                start = k * (4 * TOK) + (q * TOK + r * W2)
                return qg[:, bass.ds(start, W2)]

            third = turns_of_2 // 2
            n_chain = 4 * PIECES
            with loop(act, 0, third, per_turn + [(t, n_chain // CB) for t in loads] + [(steps, n_chain)]) as i:
                c = 0
                for a in range(2):
                    for j in range(PIECES):
                        evacuate(j)
                        for _ in range(2):
                            b = c % CB
                            hold(act, chain_in[b], loads[b].next(), held_act)
                            act.activation(piece_of(i, c), chain[:, b, :], ACT.Copy, scale=sc["g_per"]).then_inc(steps_ready, 1)
                            hold(act, steps_ready, steps.next(), held_act)
                            act.activation(chain[:, b, :], piece_of(i, c), ACT.Sigmoid,
                                           scale=sc["g_step"]).then_inc(sig_ready, 1)
                            c += 1
            act.wait_ge(scales2_ready, 1)
            act.sem_inc(act_steps, 1)
            last_act = [None]
            done2 = Tally(IC * PIECES)

            def steps_of(k, c):
                hold(act, act_done, done2.next(), held_act)
                act.activation(piece_of(k, c), chain[:, c % CB, :], ACT.Copy, scale=sc["a_fold"]).then_inc(act_steps, 1)

            with loop(act, 0, third, per_turn + [(done2, n_chain)]) as i:
                c = 0
                for a in range(2):
                    for j in range(PIECES):
                        evacuate(j)
                        for _ in range(2):
                            act.activation(chain[:, c % CB, :], piece_of(i, c), ACT.Sigmoid,
                                           scale=sc["g_step"]).then_inc(sig_ready, 1)
                            if c > 0:
                                steps_of(i, c - 1)
                            c += 1
                steps_of(i, c - 1)

        @block.gpsimd
        def _(pool):
            pool.wait_ge(joined, 1)
            pool.partition_all_reduce(sc["top"], run_peak[:, 0:1], P, REDUCE.max).then_inc(top_ready, 1)
            if up:
                pool.wait_ge(joined2, 1)
                pool.partition_all_reduce(sc["top"], act_run[:, 0:1], P, REDUCE.max).then_inc(top2_ready, 1)

        @block.vector
        def _(dve):
            done = Tally()

            def link(ins):
                ins.then_inc(dve_step, 1)
                dve.wait_ge(dve_step, done.next())

            pieces = Tally()
            if not up:
                dve.tensor_copy(run_peak[:, 0:1], keep["x2_peak"][:, :]).then_inc(joined, 1)
                dve.wait_ge(top_ready, 1)
                quantum(dve, link, sc, "x")
                link(dve.tensor_tensor(sc["g_back"], sc["x_step"], keep["half"][:, MG:MG + 1], ALU.mult))
                link(dve.memset(run_peak[:, :], 0.0))
                dve.tensor_tensor(sc["u_back"], sc["x_step"], keep["half"][:, MU:MU + 1], ALU.mult).then_inc(scales_ready, 1)
                for n in range(NG):
                    dve.wait_ge(xt_loaded[n % 2], 16 * (N // SEQ) * (n // 2 + 1))
                    if n > 0:
                        dve.wait_ge(xq_ready, n)
                    link(dve.tensor_scalar(x_steps[:, :, :], xt_in[:, n % 2], sc["x_per"], None, ALU.mult))
                    link(dve.tensor_copy(xq[:, 0, n], x_steps[:, :, :]))
                    dve.tensor_tensor(xq[:, 1, n], x_steps[:, :, :], xq[:, 0, n], ALU.subtract).then_inc(xq_ready, 1)
            else:
                link(dve.tensor_reduce(run_peak[:, 0:1], run_peak[:, :], AX.X, ALU.max))
                link(dve.memset(act_run[:, :], 0.0))
                dve.tensor_copy(act_run[:, 0:1], act_run[:, 0:1]).then_inc(joined, 1)
                dve.wait_ge(top_ready, 1)
                link(dve.memset(run_peak[:, :], 0.0))
                quantum(dve, link, sc, "g")
                dve.tensor_scalar(sc["a_unit"], sc["g_step"], 1.0 / SIG, None, ALU.mult).then_inc(scales_ready, 1)
                dve.wait_ge(scales_ready, 1)

            def peak_of(a, j):
                dve.wait_ge(staged, pieces.next())
                dve.tensor_reduce(peaks[:, a * PIECES + j:a * PIECES + j + 1], stage[:, j % ST, :], AX.X, ALU.max,
                                  apply_absolute_value=True).then_inc(peaked, 1)

            all_peaks = Tally(ST)

            def join():
                for _ in range(2 * PIECES):
                    all_peaks.next()
                dve.wait_ge(peaked, all_peaks.value)
                link(dve.tensor_tensor(run_peak[:, :], run_peak[:, :], peaks[:, :], ALU.max))

            per_turn = [(pieces, 2 * PIECES), (all_peaks, 2 * PIECES)]
            if not up:
                with loop(dve, 0, turns_of_2, per_turn + [(done, 1)]):
                    for a in range(2):
                        for j in range(PIECES):
                            peak_of(a, j)
                    join()
                return

            sigs, acts, freed = Tally(), Tally(), Tally()

            def piece_of(k, c):
                q, r = divmod(c, PIECES)
                return qg[:, bass.ds(k * (4 * TOK) + (q * TOK + r * W2), W2)]

            third = turns_of_2 // 2
            n_chain = 4 * PIECES
            with loop(dve, 0, third, per_turn + [(done, 2 * n_chain + 2), (sigs, n_chain), (acts, n_chain)]) as i:
                c = 0
                for a in range(2):
                    for j in range(PIECES):
                        peak_of(a, j)
                        for _ in range(2):
                            b = c % CB
                            dve.wait_ge(sig_ready, sigs.next())
                            link(dve.tensor_scalar(sig_steps[:, :], chain[:, b, :], SIG, SIG - 1.0, ALU.mult, ALU.min))
                            link(dve.tensor_tensor(chain[:, b, :], piece_of(i, c), sig_steps[:, :], ALU.mult))
                            dve.tensor_reduce(act_peaks[:, c:c + 1], chain[:, b, :], AX.X, ALU.max,
                                              apply_absolute_value=True).then_inc(act_done, 1)
                            acts.next()
                            c += 1
                dve.wait_ge(act_done, acts.value)
                link(dve.tensor_tensor(act_run[:, :], act_run[:, :], act_peaks[:, :], ALU.max))
                join()
            link(dve.tensor_reduce(act_run[:, 0:1], act_run[:, :], AX.X, ALU.max))
            dve.tensor_copy(act_run[:, 1:2], act_run[:, 0:1]).then_inc(joined2, 1)
            dve.wait_ge(top2_ready, 1)
            quantum(dve, link, sc, "a", unit=sc["a_unit"])
            dve.tensor_tensor(sc["a_fold"], sc["a_unit"], sc["a_per"], ALU.mult).then_inc(scales2_ready, 1)
            written = Tally(IC * PIECES)
            with loop(dve, 0, third, per_turn + [(done, n_chain + 1), (sigs, n_chain), (written, n_chain)]) as i:
                c = 0
                for a in range(2):
                    for j in range(PIECES):
                        peak_of(a, j)
                        for _ in range(2):
                            b = c % CB
                            dve.wait_ge(act_done, written.value)
                            dve.wait_ge(sig_ready, sigs.next())
                            link(dve.tensor_scalar(sig_steps[:, :], chain[:, b, :], SIG, SIG - 1.0, ALU.mult, ALU.min))
                            written.next()
                            dve.tensor_tensor(chain[:, b, :], piece_of(i, c), sig_steps[:, :],
                                              ALU.mult).then_inc(act_done, 1)
                            c += 1
                join()


def find_product_peak(nc, io, keep, sc, qg):
    CB = 4
    with ExitStack() as ctx:
        def buf(name, shape, dt):
            return ctx.enter_context(nc.sbuf_tensor("peak_" + name, shape, dt))

        def sem(name):
            return ctx.enter_context(nc.semaphore("peak_" + name))

        u = buf("u", [P, CB, W2], F32)
        u_steps = buf("u_steps", [P, 2, W2], I16)
        a_size = buf("a_size", [P, W2], I16)
        product = buf("product", [P, 2, W2], F32)
        peaks = buf("peaks", [P, PIECES], F32)
        u_in = [sem(f"u_in{b}") for b in range(CB)]
        joined, top_ready, scales_ready = sem("joined"), sem("top_ready"), sem("scales_ready")
        steps_ready, steps_used = sem("steps_ready"), sem("steps_used")
        joined2, top2_ready = sem("joined2"), sem("top2_ready")
        dve_step, held = sem("dve_step"), sem("held")
        block = ctx.enter_context(nc.Block())
        ups = io["ups"].rearrange("m p (j c) -> m p j c", c=W2)
        run_peak = keep["run_peak"]

        @block.sync
        def _(sp):
            sp.dma_start(keep["w_down"][:, :, :, :, :],
                         io["w_parts"][2 * IC:3 * IC].rearrange("u p a c o -> p u a c o")).then_inc(keep["w_down_in"], 16)
            used = Tally()
            for j in range(PIECES):
                sp.dma_start(u[:, j, :], ups[0][:, j, :]).then_inc(u_in[j], 16)
            with loop(sp, 1, IC, [(used, PIECES)]) as m:
                for j in range(PIECES):
                    sp.wait_ge(steps_ready, used.next())
                    sp.dma_start(u[:, j, :], row(ups, m)[:, j, :]).then_inc(u_in[j], 16)
            sp.wait_ge(keep["w_down_in"], 16)

        @block.scalar
        def _(act):
            act.sem_inc(steps_used, 2)
            act.wait_ge(scales_ready, 1)
            loads, free = [Tally(by=16) for _ in range(CB)], Tally()
            with loop(act, 0, IC, [(t, 1) for t in loads] + [(free, PIECES)]) as m:
                for j in range(PIECES):
                    act.wait_ge(u_in[j], loads[j].next())
                    act.wait_ge(steps_used, free.next())
                    if j % 2:
                        act.activation(u_steps[:, 1, :], u[:, j, :], ACT.Copy, scale=sc["u_per"]).then_inc(steps_ready, 1)
                    else:
                        act.activation(u_steps[:, 0, :], u[:, j, :], ACT.Abs, scale=sc["u_per"])
                        act.activation(a_size[:, :], qg[:, bass.ds(m * TOK + j * W2, W2)], ACT.Abs).then_inc(steps_ready, 1)

        @block.gpsimd
        def _(pool):
            pool.wait_ge(joined, 1)
            pool.partition_all_reduce(sc["top"], run_peak[:, 0:1], P, REDUCE.max).then_inc(top_ready, 1)
            pool.wait_ge(joined2, 1)
            pool.partition_all_reduce(sc["top"], run_peak[:, 0:1], P, REDUCE.max).then_inc(top2_ready, 1)

        @block.vector
        def _(dve):
            done = Tally()

            def link(ins):
                ins.then_inc(dve_step, 1)
                dve.wait_ge(dve_step, done.next())

            link(dve.tensor_reduce(run_peak[:, 0:1], run_peak[:, :], AX.X, ALU.max))
            dve.tensor_copy(run_peak[:, 1:2], run_peak[:, 0:1]).then_inc(joined, 1)
            dve.wait_ge(top_ready, 1)
            link(dve.memset(run_peak[:, :], 0.0))
            quantum(dve, link, sc, "u")
            dve.tensor_tensor(sc["o_unit"], sc["a_step"], sc["u_step"], ALU.mult).then_inc(scales_ready, 1)
            ready = Tally()
            with loop(dve, 0, IC, [(done, PIECES // 2 + 1), (ready, PIECES)]) as m:
                for j in range(PIECES):
                    dve.wait_ge(steps_ready, ready.next())
                    dve.wait_ge(steps_used, ready.value)
                    if j % 2 == 0:
                        dve.sem_inc(held, 1)
                    if j % 2:
                        link(dve.tensor_tensor(product[:, 1, :], qg[:, bass.ds(m * TOK + j * W2, W2)], u_steps[:, 1, :],
                                               ALU.mult))
                        dve.tensor_reduce(peaks[:, j:j + 1], product[:, 1, :], AX.X, ALU.max,
                                          apply_absolute_value=True).then_inc(steps_used, 1)
                    else:
                        dve.tensor_tensor_reduce(out=product[:, 0, :], in0=a_size[:, :], in1=u_steps[:, 0, :], scale=1.0,
                                                 scalar=0.0, op0=ALU.mult, op1=ALU.max,
                                                 accum_out=peaks[:, j:j + 1]).then_inc(steps_used, 1)
                dve.wait_ge(steps_used, ready.value + 2)
                link(dve.tensor_tensor(run_peak[:, 0:PIECES], run_peak[:, 0:PIECES], peaks[:, :], ALU.max))
            link(dve.tensor_reduce(run_peak[:, 0:1], run_peak[:, 0:PIECES], AX.X, ALU.max))
            dve.tensor_copy(run_peak[:, 1:2], run_peak[:, 0:1]).then_inc(joined2, 1)
            dve.wait_ge(top2_ready, 1)
            quantum(dve, link, sc, "o", unit=sc["o_unit"])
            link(dve.tensor_tensor(sc["o_fold"], sc["o_unit"], sc["o_per"], ALU.mult))
            link(dve.tensor_tensor(sc["d_back"], sc["o_step"], keep["half"][:, MD:MD + 1], ALU.mult))


def project_down(nc, io, keep, sc, qg):
    PR = IC // 2
    UB = 3
    TG = N // P
    with ExitStack() as ctx:
        def buf(name, shape, dt):
            return ctx.enter_context(nc.sbuf_tensor("down_" + name, shape, dt))

        def sem(name):
            return ctx.enter_context(nc.semaphore("down_" + name))

        u = buf("u", [P, UB, 2, N], F32)
        u_steps = buf("u_steps", [P, 2, 2, N], I16)
        product = buf("product", [P, 2, 2, N], F32)
        o_steps = buf("o_steps", [P, 2, 2, N], I16)
        oq = buf("oq", [P, 2, 2, IC, N], F16)
        y = buf("y", [P, TG, D], F32)
        banks = ctx.enter_context(nc.psum_tensor("down_banks", [P, TG, D], F32))
        u_in = [sem(f"u_in{b}") for b in range(UB)]
        x2_loaded = [sem(f"x2_loaded{t}") for t in range(TG)]
        y_stored = [sem(f"y_stored{t}") for t in range(TG)]
        u_ready, multiplied, o_ready, split = sem("u_ready"), sem("multiplied"), sem("o_ready"), sem("split")
        filled, summed = sem("filled"), sem("summed")
        dve_step = sem("dve_step")
        block = ctx.enter_context(nc.Block())
        ups = io["ups"].rearrange("(q a) p (n c) -> n q p a c", a=2, c=N)
        x2_tiles = io["x2"].rearrange("b (t p) d -> (b t) p d", p=P)
        out_tiles = io["out"].rearrange("b (t p) d -> (b t) p d", p=P)
        w_down = keep["w_down"][:, :, :, :, :].rearrange("p (r k) a c o -> p a k c r o", k=IC // DC)
        products = qg[:, :].rearrange("p (m t) -> p m t", t=TOK)

        @block.sync
        def _(sp):
            used, outs = Tally(-UB), Tally()
            stores = [Tally(-16, by=16) for _ in range(TG)]

            def load_u(n, q, first):
                if first:
                    used.next()
                else:
                    sp.wait_ge(u_ready, used.next())
                sp.dma_start(u[:, q % UB], row(ups[:, q], n)).then_inc(u_in[q % UB], 16)

            def load_x2(n, t, first):
                if first:
                    stores[t].next()
                else:
                    sp.wait_ge(y_stored[t], stores[t].next())
                sp.dma_start(y[:, t, :], row(x2_tiles, n * TG + t)).then_inc(x2_loaded[t], 16)

            def store(n, t):
                sp.wait_ge(summed, outs.next())
                sp.dma_start(row(out_tiles, n * TG + t), y[:, t, :]).then_inc(y_stored[t], 16)

            def group(n, start, before, before2):
                for q in range(PR):
                    load_u(n, q, start == 0 and q < UB)
                    if q < 2 and before2:
                        store(n - 2, 2 + q)
                    if q in (2, 3) and before:
                        load_x2(n - 1, 2 * (q - 2), start == 1)
                        load_x2(n - 1, 2 * (q - 2) + 1, start == 1)
                    if q > 3 and before:
                        store(n - 1, q - 4)

            group(0, 0, False, False)
            group(1, 1, True, False)
            with loop(sp, 1, NG // 2, [(used, 2 * PR), (outs, 2 * TG)] + [(t, 2) for t in stores]) as k:
                group(k * 2, 2, True, True)
                group(k * 2 + 1, 3, True, True)
            for t in (2, 3):
                store(NG - 2, t)
            for t in range(TG):
                load_x2(NG - 1, t, False)
            for t in range(TG):
                store(NG - 1, t)
            for t in range(TG):
                sp.wait_ge(y_stored[t], 16 * NG)

        @block.scalar
        def _(act):
            loads = [Tally(by=16) for _ in range(UB)]
            free_u, made, free_o = Tally(-2), Tally(), Tally(-2)

            def u_of(q, first):
                b = q % UB
                act.wait_ge(u_in[b], loads[b].next())
                if first:
                    free_u.next()
                else:
                    act.wait_ge(multiplied, free_u.next())
                act.activation(u_steps[:, q % 2], u[:, b], ACT.Copy, scale=sc["u_per"]).then_inc(u_ready, 1)

            def o_of(q, first):
                act.wait_ge(multiplied, made.next())
                if first:
                    free_o.next()
                else:
                    act.wait_ge(split, free_o.next())
                act.activation(o_steps[:, q % 2], product[:, q % 2], ACT.Copy, scale=sc["o_fold"]).then_inc(o_ready, 1)

            def group(first):
                for q in range(PR):
                    u_of(q, first and q < 2)
                    if q > 0:
                        o_of(q - 1, first and q - 1 < 2)
                o_of(PR - 1, False)

            group(True)
            group(False)
            with loop(act, 1, NG // 2, [(t, 2 * PR // UB) for t in loads] + [(t, 2 * PR) for t in (free_u, made, free_o)]):
                group(False)
                group(False)

        @block.vector
        def _(dve):
            us, os, done = Tally(), Tally(), Tally()
            free_p = Tally(-2)
            fills, x2s = Tally(), [Tally(by=16) for _ in range(TG)]

            def link(ins):
                ins.then_inc(dve_step, 1)
                dve.wait_ge(dve_step, done.next())

            def multiply(n, q, first):
                dve.wait_ge(u_ready, us.next())
                if first:
                    free_p.next()
                else:
                    dve.wait_ge(o_ready, free_p.next())
                dve.tensor_tensor(product[:, q % 2], products[:, 2 * q:2 * q + 2, bass.ds(n * N, N)], u_steps[:, q % 2],
                                  ALU.mult).then_inc(multiplied, 1)

            def parts(par, q, free):
                dve.wait_ge(o_ready, os.next())
                if free is not None:
                    dve.wait_ge(filled, free)
                link(dve.tensor_copy(oq[:, par, 0, 2 * q:2 * q + 2, :], o_steps[:, q % 2]))
                dve.tensor_tensor(oq[:, par, 1, 2 * q:2 * q + 2, :], o_steps[:, q % 2], oq[:, par, 0, 2 * q:2 * q + 2, :],
                                  ALU.subtract).then_inc(split, 1)

            def add(t):
                dve.wait_ge(filled, fills.next())
                dve.wait_ge(x2_loaded[t], x2s[t].next())
                dve.scalar_tensor_tensor(out=y[:, t, :], in0=banks[:, t, :], scalar=sc["d_back"], in1=y[:, t, :],
                                         op0=ALU.mult, op1=ALU.add).then_inc(summed, 1)

            def group(n, par, first, before, before2, free):
                for q in range(PR):
                    multiply(n, q, first and q < 2)
                    if q == 0 and before2:
                        add(TG - 1)
                    if q > 0:
                        parts(par, q - 1, free if q == 1 else None)
                    if q > 2 and before:
                        add(q - 3)
                parts(par, PR - 1, None)

            group(0, 0, True, False, False, None)
            group(1, 1, False, True, False, None)
            with loop(dve, 1, NG // 2, [(done, 2 * PR), (us, 2 * PR), (os, 2 * PR), (free_p, 2 * PR), (fills, 2 * TG)]
                      + [(t, 2) for t in x2s]) as k:
                for par in range(2):
                    group(k * 2 + par, par, False, True, True, k * (2 * TG) + (par - 1) * TG)
            add(TG - 1)
            for t in range(TG):
                add(t)

        @block.tensor
        def _(pe):
            ready, sums = Tally(), Tally(-TG)

            def group(par, first):
                for _ in range(PR):
                    ready.next()
                for t in range(TG):
                    if t == 0:
                        pe.wait_ge(split, ready.value)
                    if first:
                        sums.next()
                    else:
                        pe.wait_ge(summed, sums.next())
                    k = 0
                    for m in range(IC):
                        wk, c = divmod(m, DC)
                        for op, wp in ((0, 0), (1, 0), (0, 1)):
                            last = pe.matmul(banks[:, t, :], oq[:, par, op, m, t * P:(t + 1) * P], w_down[:, wp, wk, c],
                                             start=(k == 0), stop=(k == 3 * IC - 1))
                            k += 1
                    last.then_inc(filled, 1)

            group(0, True)
            group(1, False)
            with loop(pe, 1, NG // 2, [(ready, 2 * PR), (sums, 2 * TG)]):
                group(0, False)
                group(1, False)


def feed_forward(nc, io, keep):
    with ExitStack() as ctx:
        def buf(name, shape, dt):
            return ctx.enter_context(nc.sbuf_tensor(name, shape, dt))

        sc = Scales(buf("ffn_scales", [P, len(Scales.names)], F32))
        keep["run_peak"] = buf("run_peak", [P, 2 * PIECES], F32)
        keep["act_peak"] = buf("act_peak", [P, 4 * PIECES], F32)
        keep["w_down_in"] = ctx.enter_context(nc.semaphore("w_down_in"))
        qg = buf("qg", [P, IC * TOK], I16)
        with ExitStack() as wide:
            xq = wide.enter_context(nc.sbuf_tensor("xq", [P, 2, NG, DC, N], F16))
            project(nc, io, keep, sc, xq, qg, "gate")
            project(nc, io, keep, sc, xq, qg, "up")
        keep["w_down"] = buf("w_down", [P, IC, 2, DC, P], F16)
        find_product_peak(nc, io, keep, sc, qg)
        project_down(nc, io, keep, sc, qg)


def build(nc, io):
    def scratch(name, shape, dt):
        return nc.dram_tensor(name + "_dram", shape, dt, kind="Internal").ap()

    io["w_parts"] = scratch("w_parts", (3 * IC, P, 2, DC, P), F16)
    io["x2"] = scratch("x2", (BATCH, SEQ, D), F32)
    io["xt2"] = scratch("xt2", (BATCH, P, DC, SEQ), F32)
    io["gates"] = scratch("gates", (IC, P, TOK), F32)
    io["ups"] = scratch("ups", (IC, P, TOK), F32)
    with ExitStack() as ctx:
        keep = {
            "half": ctx.enter_context(nc.sbuf_tensor("half", [P, 8], F32)),
            "x2_peak": ctx.enter_context(nc.sbuf_tensor("x2_peak", [P, 1], F32)),
        }
        with ExitStack() as first:
            def buf(name, shape, dt):
                keep[name] = first.enter_context(nc.sbuf_tensor(name, shape, dt))

            buf("ident", [P, P], F32)
            buf("ident_b", [P, P], BF16)
            buf("mask", [P, 2 * P], BF16)
            buf("minus_half", [P, TT], F32)
            buf("inv", [P, 8], F32)
            buf("back", [P, 3], F32)
            buf("cos", [P, SEQ], F32)
            buf("sin", [P, SEQ], F32)
            buf("bqk", [P, 2 * DC], F32)
            buf("bv", [P, DC], F32)
            buf("bias_row", [P, D], F32)
            buf("attn_hi", [P, 4, DC, D], F16)
            buf("attn_lo", [P, 4, DC, D], F16)
            prepare(nc, io, keep)
            attend(nc, io, keep)
        feed_forward(nc, io, keep)


def kernel(x, ctx_1024, L0_xattn_Wq, L0_xattn_bq, L0_xattn_Wk, L0_xattn_bk, L0_xattn_Wv, L0_xattn_bv,
           L0_xattn_Wo, L0_xattn_bo, L0_ffn_w_gate, L0_ffn_w_up, L0_ffn_w_down):
    import numpy as np
    import concourse.bacc as bacc
    from concourse.bass_utils import run_bass_kernel_spmd as run

    half = HD // 2
    freq = (1.0 / 10000.0 ** (np.arange(half, dtype=np.float32) / np.float32(half))).astype(np.float32)
    angle = (np.arange(SEQ, dtype=np.float32)[None, :] * freq[:, None]).astype(np.float32)
    cos, sin = np.cos(angle), np.sin(angle)
    heads = P // HD
    units = lambda w: np.asarray(w).reshape(-1, P, D)
    arrays = {
        "x": np.asarray(x),
        "ctx": np.asarray(ctx_1024),
        "attn_w": np.concatenate([units(L0_xattn_Wq), units(L0_xattn_Wk), units(L0_xattn_Wv), units(L0_xattn_Wo)]),
        "ffn_w": np.concatenate([units(L0_ffn_w_gate), units(L0_ffn_w_up),
                                 np.asarray(L0_ffn_w_down).reshape(DC, P, INNER // D, D).transpose(0, 2, 1, 3)
                                 .reshape(IC, P, D)]),
        "bqk": np.concatenate([np.asarray(L0_xattn_bq).reshape(DC, P), np.asarray(L0_xattn_bk).reshape(DC, P)]).T,
        "bv": np.asarray(L0_xattn_bv).reshape(DC, P).T,
        "bias_row": np.broadcast_to(np.asarray(L0_xattn_bo), (P, D)),
        "cos": np.tile(np.concatenate([cos, cos]), (heads, 1)),
        "sin": np.tile(np.concatenate([sin, -sin]), (heads, 1)),
    }
    arrays = {k: np.ascontiguousarray(v) for k, v in arrays.items()}
    nc = bacc.Bacc("TRN2", target_bir_lowering=False, num_devices=1)
    io = {k: nc.dram_tensor(f"in_{k}", v.shape, F32, kind="ExternalInput").ap() for k, v in arrays.items()}
    io["out"] = nc.dram_tensor("out_y", (BATCH, SEQ, D), F32, kind="ExternalOutput").ap()
    build(nc, io)
    r = run(nc, [{f"in_{k}": v for k, v in arrays.items()}], core_ids=[0])
    return r.results[0]["out_y"]
```

```python
from contextlib import ExitStack, contextmanager

import concourse.bass as bass
from concourse import mybir

ALU = mybir.AluOpType
ACT = mybir.ActivationFunctionType
AX = mybir.AxisListType
F32 = mybir.dt.float32
F16 = mybir.dt.float16
BF16 = mybir.dt.bfloat16
I32 = mybir.dt.int32
I16 = mybir.dt.int16
U16 = mybir.dt.uint16
REDUCE = bass.bass_isa.ReduceOp

P = 128
BATCH, SEQ, D = 16, 256, 512
HEADS, HD = 16, 32
INNER = 1536
DC = D // P
TT = SEQ // P
IC = INNER // P
HG = P // HD
GROUPS = HEADS // HG
QBLOCK = 32
LN_EPS = 1e-5
STEP_FLOOR = 1e-12
TINY = 1e-30
EXPONENT = 0x7F800000
MAGIC = 1.5 * 2.0 ** 23
SCORE_SCALE = float(HD) ** -0.5
MASKED = -1e30
WMAX = 7.0
QMAX = 32767.0
SIG = 65536.0
HALF_TURN = [(k + HD // 2) % HD for k in range(HD)]
MATS = ("q", "k", "v", "o", "gate", "up", "down", "ctx")
MQ, MK, MV, MO, MG, MU, MD, MC = range(8)


class Tally:

    def __init__(self, start=0, by=1):
        self.value, self.by, self.made = start, by, 0

    def next(self):
        self.made += 1
        self.value = self.value + self.by
        return self.value


class Ring:

    def __init__(self, banks):
        self.banks, self.at = banks, 0
        self.fills = [Tally() for _ in range(banks)]

    def next(self):
        b = self.at % self.banks
        self.at += 1
        return b, self.fills[b].next()

    def back(self, k):
        b = (self.at - k) % self.banks
        return b, self.fills[b].value


@contextmanager
def loop(eng, lo, hi, tallies):
    start = [t.value for t, _ in tallies]
    with eng.Fori(lo, hi) as i:
        for (t, n), v in zip(tallies, start):
            t.value, t.made = v + (i - lo) * (t.by * n), 0
        yield i
        for k, (t, n) in enumerate(tallies):
            assert t.made == n, ("tally", k, "made", t.made, "said", n)
    for (t, n), v in zip(tallies, start):
        t.value = v + t.by * n * (hi - lo)


def row(view, i):
    if isinstance(i, int):
        return view[i]
    v = view[bass.ds(i, 1)]
    names = "abcd"[: len(v.shape) - 2]
    return v.rearrange(f"z p {' '.join(names)} -> (z p) {' '.join(names)}")


def split_scales(dve, link, dst_inv, dst_half, peak, power):
    link(dve.tensor_scalar(peak, peak, TINY, None, ALU.max))
    link(dve.tensor_scalar(power.bitcast(I32), peak.bitcast(I32), EXPONENT, None, ALU.bitwise_and))
    link(dve.tensor_scalar(dst_inv.bitcast(I32), power.bitcast(I32), EXPONENT, None, ALU.bitwise_xor))
    link(dve.tensor_scalar(dst_half, power, 0.5, None, ALU.mult))


def prepare(nc, io, keep):
    CH, RB = 4, 4
    n_ffn, n_ctx = 3 * IC // CH, BATCH * TT // CH
    n_peak = 4 + n_ffn + n_ctx
    with ExitStack() as ctx:
        def buf(name, shape, dt):
            return ctx.enter_context(nc.sbuf_tensor(name, shape, dt))

        def sem(name):
            return ctx.enter_context(nc.semaphore(name))

        raw_attn = buf("raw_attn", [P, 4 * CH, D], F32)
        raw = buf("raw", [P, RB, CH, D], F32)
        peak = buf("peak", [P, n_peak], F32)
        peak8 = buf("peak8", [P, 8], F32)
        top8 = buf("top8", [P, 8], F32)
        power8 = buf("power8", [P, 8], F32)
        ffn_peak = buf("ffn_peak", [P, 3], F32)
        ffn_top = buf("ffn_top", [P, 3], F32)
        ffn_power = buf("ffn_power", [P, 3], F32)
        wo32 = buf("wo32", [P, DC, D], F32)
        bv_cols = buf("bv_cols", [P, DC, P], F32)
        ones = buf("ones", [P, P], F32)
        banks = ctx.enter_context(nc.psum_tensor("prep_banks", [P, 4, D], F32))
        bias_bank = ctx.enter_context(nc.psum_tensor("bias_bank", [P, D], F32))

        attn_in = [sem(f"attn_in{k}") for k in range(4)]
        raw_in = [sem(f"raw_in{k}") for k in range(RB)]
        const_in = sem("const_in")
        peak_done = sem("peak_done")
        peaks_joined = sem("peaks_joined")
        top_ready = sem("top_ready")
        dve_step = sem("dve_step")
        scales_ready = sem("scales_ready")
        pool_step = sem("pool_step")
        ident_ready = sem("ident_ready")
        turned = sem("turned")
        hi_ready = sem("hi_ready")
        lo_ready = sem("lo_ready")
        wo_ready = sem("wo_ready")
        bv_ready = sem("bv_ready")
        bias_sum = sem("bias_sum")
        block = ctx.enter_context(nc.Block())

        ffn_loads = io["ffn_w"].rearrange("(m u) p d -> m p u d", u=CH)
        attn_loads = io["attn_w"].rearrange("(m u) p d -> m p u d", u=CH)
        ctx_loads = io["ctx"].rearrange("b (t p) d -> p (b t) d", p=P)
        @block.sync
        def _(sp):
            for k in range(4):
                sp.dma_start(raw_attn[:, k * CH:(k + 1) * CH, :], attn_loads[k]).then_inc(attn_in[k], 16)
            for name in ("cos", "sin", "bqk", "bv", "bias_row"):
                sp.dma_start(keep[name][:, :], io[name]).then_inc(const_in, 16)
            for k in range(n_ctx + n_ffn):
                if k >= RB:
                    sp.wait_ge(peak_done, 4 + k - RB + 1)
                src = ctx_loads[:, k * CH:(k + 1) * CH, :] if k < n_ctx else ffn_loads[k - n_ctx]
                sp.dma_start(raw[:, k % RB, :, :], src).then_inc(raw_in[k % RB], 16)

        @block.gpsimd
        def _(pool):
            pool.memset(keep["ident"][:, :], 0.0).then_inc(pool_step, 1)
            pool.memset(keep["ident_b"][:, :], 0.0).then_inc(pool_step, 1)
            pool.memset(keep["mask"][:, :], 0.0).then_inc(pool_step, 1)
            pool.memset(keep["minus_half"][:, :], -0.5).then_inc(pool_step, 1)
            pool.memset(ones[:, :], 1.0).then_inc(pool_step, 1)
            pool.wait_ge(pool_step, 5)
            for name in ("ident", "ident_b"):
                pool.affine_select(out=keep[name][:, :], in_=keep[name][:, :], compare_op=ALU.not_equal, fill=1.0,
                                   base=0, pattern=[[-1, P]], channel_multiplier=1).then_inc(ident_ready, 1)
            for at in (0, P):
                diag = keep["mask"][:, at:at + P]
                pool.affine_select(out=diag, in_=diag, compare_op=ALU.is_ge, fill=MASKED,
                                   base=0, pattern=[[-1, P]], channel_multiplier=1).then_inc(ident_ready, 1)
            pool.wait_ge(peaks_joined, 1)
            pool.partition_all_reduce(top8[:, :], peak8[:, :], P, REDUCE.max).then_inc(top_ready, 1)
            pool.wait_ge(peaks_joined, 2)
            pool.partition_all_reduce(ffn_top[:, :], ffn_peak[:, :], P, REDUCE.max).then_inc(top_ready, 1)

        @block.vector
        def _(dve):
            done = Tally()

            def link(ins):
                ins.then_inc(dve_step, 1)
                dve.wait_ge(dve_step, done.next())

            fills = [0] * RB

            def peaks_of(lo, hi):
                for k in range(lo, hi):
                    if k < 4:
                        dve.wait_ge(attn_in[k], 16)
                        src = raw_attn[:, k * CH:(k + 1) * CH, :]
                    else:
                        b = (k - 4) % RB
                        fills[b] += 16
                        dve.wait_ge(raw_in[b], fills[b])
                        src = raw[:, b, :, :]
                    dve.tensor_reduce(peak[:, k:k + 1], src, AX.XY, ALU.max,
                                      apply_absolute_value=True).then_inc(peak_done, 1)

            peaks_of(0, 4 + n_ctx)
            dve.wait_ge(peak_done, 4 + n_ctx)
            link(dve.memset(peak8[:, :], 1.0))
            dve.tensor_copy(peak8[:, 0:4], peak[:, 0:4]).then_inc(dve_step, 1)
            done.next()
            link(dve.tensor_reduce(peak8[:, 7:8], peak[:, 4:4 + n_ctx], AX.X, ALU.max))
            dve.tensor_copy(power8[:, :], peak8[:, :]).then_inc(peaks_joined, 1)
            dve.wait_ge(top_ready, 1)
            split_scales(dve, link, keep["inv"][:, :], keep["half"][:, :], top8[:, :], power8[:, :])
            half = keep["half"]
            link(dve.tensor_copy(keep["back"][:, 0:1], half[:, MQ:MQ + 1]))
            link(dve.tensor_tensor(keep["back"][:, 1:2], half[:, MK:MK + 1], half[:, MC:MC + 1], ALU.mult))
            link(dve.tensor_tensor(keep["back"][:, 2:3], half[:, MV:MV + 1], half[:, MC:MC + 1], ALU.mult))
            link(dve.tensor_tensor(keep["back"][:, 2:3], keep["back"][:, 2:3], half[:, MO:MO + 1], ALU.mult))
            link(dve.memset(keep["x2_peak"][:, :], 0.0))
            dve.wait_ge(ident_ready, 4)
            dve.wait_ge(const_in, 16 * 5)
            for c in range(DC):
                ins = dve.tensor_scalar(bv_cols[:, c, :], ones[:, :], keep["bv"][:, c:c + 1], None, ALU.mult)
                ins.then_inc(bv_ready, 1)
            dve.tensor_copy(power8[:, :], keep["inv"][:, :]).then_inc(scales_ready, 1)
            for u in range(4 * DC):
                dve.wait_ge(hi_ready, u + 1)
                m, r = u // DC, u % DC
                dve.scalar_tensor_tensor(
                    out=keep["attn_lo"][:, m, :, r * P:(r + 1) * P],
                    in0=banks[:, u % 4, :].rearrange("p (c o) -> p c o", c=DC), scalar=keep["inv"][:, m:m + 1],
                    in1=keep["attn_hi"][:, m, :, r * P:(r + 1) * P], op0=ALU.mult, op1=ALU.subtract).then_inc(lo_ready, 1)
                if u % 2 and u // 2 < n_ffn:
                    peaks_of(4 + n_ctx + u // 2, 4 + n_ctx + u // 2 + 1)
            dve.wait_ge(bias_sum, 1)
            link(dve.tensor_tensor(keep["bias_row"][:, :], keep["bias_row"][:, :], bias_bank[:, :], ALU.add))
            peaks_of(4 + n_ctx + min(2 * DC, n_ffn), n_peak)
            dve.wait_ge(peak_done, n_peak)
            link(dve.tensor_reduce(ffn_peak[:, :], peak[:, 4 + n_ctx:n_peak].rearrange("p (m k) -> p m k", k=IC // CH),
                                   AX.X, ALU.max))
            dve.tensor_copy(ffn_power[:, :], ffn_peak[:, :]).then_inc(peaks_joined, 1)
            dve.wait_ge(top_ready, 2)
            split_scales(dve, link, keep["inv"][:, MG:MD + 1], keep["half"][:, MG:MD + 1], ffn_top[:, :], ffn_power[:, :])


        @block.tensor
        def _(pe):
            pe.wait_ge(ident_ready, 2)
            for u in range(4 * DC):
                if u >= 4:
                    pe.wait_ge(lo_ready, u - 3)
                if u == 0:
                    for k in range(4):
                        pe.wait_ge(attn_in[k], 16)
                for c in range(DC):
                    last = pe.transpose(banks[:, u % 4, c * P:(c + 1) * P], raw_attn[:, u, c * P:(c + 1) * P],
                                        keep["ident"][:, :])
                last.then_inc(turned, 1)
            pe.wait_ge(wo_ready, DC)
            pe.wait_ge(bv_ready, DC)
            for c in range(DC):
                last = pe.matmul(bias_bank[:, :], bv_cols[:, c, :], wo32[:, c, :], start=(c == 0), stop=(c == DC - 1))
            last.then_inc(bias_sum, 1)

        @block.scalar
        def _(act):
            act.wait_ge(scales_ready, 1)
            for u in range(4 * DC):
                act.wait_ge(turned, u + 1)
                m, r = u // DC, u % DC
                src = banks[:, u % 4, :].rearrange("p (c o) -> p c o", c=DC)
                if m == MO:
                    act.activation(wo32[:, :, r * P:(r + 1) * P], src, ACT.Copy).then_inc(wo_ready, 1)
                act.activation(keep["attn_hi"][:, m, :, r * P:(r + 1) * P], src, ACT.Copy,
                               scale=keep["inv"][:, m:m + 1]).then_inc(hi_ready, 1)


def turn_steps(i_in, nxt, nxt2, prev, weights=False):
    steps = []
    for g in range(GROUPS):
        if i_in:
            steps.append(("scores", g))
        if g == 0:
            if prev:
                steps.append(("turn_p", GROUPS - 1))
            if i_in:
                steps.append(("value", 0))
            if weights:
                steps.append(("quantise", 0))
            if prev:
                steps.append(("apply", GROUPS - 1))
            if nxt:
                steps.append(("turn", 0))
            if weights:
                steps.append(("quantise", 1))
            if prev:
                steps.append(("out", 0))
            if nxt:
                steps.append(("query_key", 0))
        else:
            if i_in:
                steps.append(("turn_p", g - 1))
            if weights:
                steps.append(("weight", g - 1))
            if nxt:
                steps.append(("query_key", g))
            if i_in:
                steps.append(("apply", g - 1))
        if g == 1 and weights:
            steps.append(("quantise", 2))
        if g == 1 and i_in:
            steps.append(("residual", 0))
        if g == 2 and prev:
            steps.append(("turn_x2", 0))
        if g == 2 and nxt2:
            steps.append(("norm", 0))
    return steps


UNITS = 3
BODY = IC // UNITS


def turns(eng, turn, tallies):
    turn(-2, turn_steps(False, False, True, False), 0)
    turn(-1, turn_steps(False, True, True, False), 1)
    turn(0, turn_steps(True, True, True, False), 0)
    middle = turn_steps(True, True, True, True)
    weighted = turn_steps(True, True, True, True, True)
    with loop(eng, 0, 3 * IC // (BODY * UNITS), [(t, BODY * n // over) for t, n, over in tallies]) as k:
        for h in range(BODY):
            turn(k * BODY + (1 + h), ([("matrix", k)] if h == 0 else []) + weighted, (1 + h) % 2)
    turn(BATCH - 3, middle, 1)
    turn(BATCH - 2, turn_steps(True, True, False, True), 0)
    turn(BATCH - 1, turn_steps(True, False, False, True), 1)
    turn(BATCH, turn_steps(False, False, False, True), 0)


def attend(nc, io, keep):
    RING = 4
    FILLS = 4 * GROUPS + TT + 2 * TT + TT + GROUPS + TT + UNITS
    with ExitStack() as ctx:
        def buf(name, shape, dt):
            return ctx.enter_context(nc.sbuf_tensor(name, shape, dt))

        def sem(name):
            return ctx.enter_context(nc.semaphore(name))

        x_in = buf("x_in", [P, TT, D], F32)
        c_in = buf("c_in", [P, TT, D], F32)
        x_res = buf("x_res", [P, TT, D], F32)
        xb = buf("xb", [P, TT, D], F32)
        stats = buf("stats", [P, TT, 6], F32)
        mean = buf("mean", [P, TT], F32)
        half_gap = buf("half_gap", [P, TT], F32)
        spread = buf("spread", [P, TT], F32)
        var_eps = buf("var_eps", [P, TT], F32)
        rstd = buf("rstd", [P, TT], F32)
        xn = buf("xn", [P, TT, D], F32)
        xt = buf("xt", [P, 2, DC, SEQ], F16)
        ct = buf("ct", [P, 2, DC, SEQ], F16)
        raw = buf("raw_qk", [P, 2, 2, SEQ], F32)
        by_sin = buf("by_sin", [P, 2, SEQ], F32)
        by_cos = buf("by_cos", [P, 2, SEQ], F32)
        sin_turned = buf("sin_turned", [P, 2, SEQ], F32)
        qk = buf("qk", [P, GROUPS, 2, SEQ], F32)
        v = buf("v", [P, 2, TT, D], F32)
        neg_max = buf("neg_max", [P, 2, HG], F32)
        prob = buf("prob", [P, 2, HG, 3 * P], F32)
        row_sum = buf("row_sum", [P, 2, 2, HG], F32)
        per_sum = buf("per_sum", [P, 2, 2, HG], F32)
        pt0 = buf("pt0", [P, HG, SEQ], F32)
        pt1 = buf("pt1", [P, HG, P], F32)
        ot = buf("ot", [P, 2, GROUPS, SEQ], F16)
        x2 = buf("x2", [P, TT, D], F32)
        stats2 = buf("stats2", [P, TT, 6], F32)
        mean2 = buf("mean2", [P, TT], F32)
        var_eps2 = buf("var_eps2", [P, TT], F32)
        rstd2 = buf("rstd2", [P, TT], F32)
        xn2 = buf("xn2", [P, TT, D], F32)
        xn2_peak = buf("xn2_peak", [P, 1], F32)
        xt2 = buf("xt2", [P, DC, SEQ], F32)
        w_raw = buf("w_raw", [P, UNITS, D], F32)
        w_deq = buf("w_deq", [P, UNITS, D], F32)
        block_max = buf("block_max", [P, D // QBLOCK], F32)
        step = buf("step", [P, UNITS, D // QBLOCK], F32)
        per_step = buf("per_step", [P, D // QBLOCK], F32)
        inv_now = buf("inv_now", [P, 1], F32)
        parts = buf("parts", [P, UNITS, 2, DC, P], F16)
        score_banks = ctx.enter_context(nc.psum_tensor("score_banks", [P, HG, D], F32))
        banks = ctx.enter_context(nc.psum_tensor("ring_banks", [P, RING, D], F32))

        x_loaded, c_loaded, res_loaded = sem("x_loaded"), sem("c_loaded"), sem("res_loaded")
        x2_stored, xt2_stored = sem("x2_stored"), sem("xt2_stored")
        var_ready, rstd_ready = sem("var_ready"), sem("rstd_ready")
        var2_ready, rstd2_ready = sem("var2_ready"), sem("rstd2_ready")
        xn_ready = sem("xn_ready")
        xb_ready, x2_ready, xn2_ready = sem("xb_ready"), sem("x2_ready"), sem("xn2_ready")
        filled = [sem(f"filled{b}") for b in range(RING)]
        emptied = [sem(f"emptied{b}") for b in range(RING)]
        turn_hi, heads_hi = sem("turn_hi"), sem("heads_hi")
        raw_used, rotated = sem("raw_used"), sem("rotated")
        scored, max_ready, exped, sums_ready = sem("scored"), sem("max_ready"), sem("exped"), sem("sums_ready")
        normed = sem("normed")
        w_in = [sem(f"w_in{k}") for k in range(UNITS)]
        w_rounded, w_hi = sem("w_rounded"), sem("w_hi")
        w_quantised = sem("w_quantised")
        parts_stored = [sem(f"parts_stored{k}") for k in range(UNITS)]
        dve_step = sem("attn_dve_step")
        block = ctx.enter_context(nc.Block())

        x_tiles = io["x"].rearrange("b (t p) d -> b p t d", p=P)
        c_tiles = io["ctx"].rearrange("b (t p) d -> b p t d", p=P)
        x2_tiles = io["x2"].rearrange("b (t p) d -> b p t d", p=P)

        @block.sync
        def _(sp):
            def turn(i, steps, par):
                names = [s for s, _ in steps]
                if "weight" in names:
                    for k in range(UNITS):
                        sp.wait_ge(w_quantised, (i - 1) * UNITS + (k + 1))
                        sp.dma_start(w_raw[:, k, :], row(io["ffn_w"], (i - 1) * UNITS + k)).then_inc(w_in[k], 16)
                if "norm" in names:
                    if not isinstance(i, int) or i + 2 > 0:
                        sp.wait_ge(xn_ready, i + 2)
                    sp.dma_start(x_in[:, :, :], row(x_tiles, i + 2)).then_inc(x_loaded, 16)
                if "residual" in names:
                    if not isinstance(i, int) or i > 0:
                        sp.wait_ge(xb_ready, i)
                    sp.dma_start(x_res[:, :, :], row(x_tiles, i)).then_inc(res_loaded, 16)
                if "norm" in names:
                    if not isinstance(i, int) or i + 2 > 0:
                        sp.wait_ge(turn_hi, i * (2 * TT) + 4 * TT)
                    sp.dma_start(c_in[:, :, :], row(c_tiles, i + 2)).then_inc(c_loaded, 16)
                if "out" in names:
                    sp.wait_ge(x2_ready, TT * i)
                    sp.dma_start(row(x2_tiles, i - 1), x2[:, :, :]).then_inc(x2_stored, 16)
                last = fills_of(steps)
                if "out" in names:
                    b, n = last["turn_x2", 0]
                    sp.wait_ge(emptied[b], n + 1)
                    sp.dma_start(row(io["xt2"], i - 1), xt2[:, :, :]).then_inc(xt2_stored, 16)
                if "weight" in names:
                    for k in range(UNITS):
                        b, n = last["weight", k]
                        sp.wait_ge(emptied[b], n + 1)
                        sp.dma_start(row(io["w_parts"], (i - 1) * UNITS + k), parts[:, k]).then_inc(parts_stored[k], 16)

            ring = Ring(RING)

            def fills_of(steps):
                count = {"turn_p": 3, "apply": 1, "value": TT, "turn": 2 * TT, "out": TT, "query_key": 1, "turn_x2": TT,
                         "weight": 1}
                last = {}
                for s, g in steps:
                    for _ in range(count.get(s, 0)):
                        last[s, g if s == "weight" else 0] = ring.next()
                return last

            turns(sp, turn, [(f, FILLS, RING) for f in ring.fills])
            sp.wait_ge(x2_stored, 16 * BATCH)
            sp.wait_ge(xt2_stored, 16 * BATCH)
            for k in range(UNITS):
                sp.wait_ge(parts_stored[k], 16 * (3 * IC // UNITS + 1))

        @block.gpsimd
        def _(pool):
            def turn(i, steps, par):
                for s, g in steps:
                    if s == "norm":
                        pool.wait_ge(var_ready, i + 3)
                        pool.tensor_tensor(rstd[:, :], var_eps[:, :], keep["minus_half"][:, :],
                                           ALU.pow).then_inc(rstd_ready, 1)
                    if s == "out":
                        pool.wait_ge(var2_ready, i)
                        pool.tensor_tensor(rstd2[:, :], var_eps2[:, :], keep["minus_half"][:, :],
                                           ALU.pow).then_inc(rstd2_ready, 1)
                    if s == "quantise":
                        pool.wait_ge(w_rounded, (i - 1) * UNITS + (g + 1))
                        q = w_deq[:, g, :].rearrange("p (k j) -> p k j", j=QBLOCK)
                        pool.tensor_tensor(q, q, step[:, g, :].unsqueeze(2).to_broadcast([P, D // QBLOCK, QBLOCK]),
                                           ALU.mult).then_inc(w_quantised, 1)
                    if s == "residual":
                        pool.wait_ge(res_loaded, i * 16 + 16)
                        if not isinstance(i, int) or i > 0:
                            pool.wait_ge(x2_ready, i * TT)
                        pool.tensor_tensor(xb[:, :, :], x_res[:, :, :],
                                           keep["bias_row"][:, :].unsqueeze(1).to_broadcast([P, TT, D]),
                                           ALU.add).then_inc(xb_ready, 1)
                    if s == "scores":
                        pool.wait_ge(sums_ready, i * GROUPS + (g + 1))
                        pr, ps = prob[:, g % 2], per_sum[:, g % 2]
                        pool.tensor_tensor(pr[:, :, 0:P], pr[:, :, 0:P],
                                           ps[:, 0, :].unsqueeze(2).to_broadcast([P, HG, P]), ALU.mult)
                        pool.tensor_tensor(pr[:, :, P:3 * P], pr[:, :, P:3 * P],
                                           ps[:, 1, :].unsqueeze(2).to_broadcast([P, HG, 2 * P]),
                                           ALU.mult).then_inc(normed, 1)

            turns(pool, turn, [])

        @block.vector
        def _(dve):
            ring = Ring(RING)
            done = Tally()

            def link(ins):
                ins.then_inc(dve_step, 1)
                dve.wait_ge(dve_step, done.next())

            def mean_and_var(st, mean, var_eps):
                dve.tensor_tensor(mean[:, :], st[:, :, 1], st[:, :, 4], ALU.add).then_inc(dve_step, 1)
                done.next()
                dve.tensor_tensor(half_gap[:, :], st[:, :, 1], st[:, :, 4], ALU.subtract).then_inc(dve_step, 1)
                done.next()
                link(dve.tensor_tensor(spread[:, :], st[:, :, 2], st[:, :, 5], ALU.add))
                dve.tensor_scalar(mean[:, :], mean[:, :], 0.5, None, ALU.mult).then_inc(dve_step, 1)
                done.next()
                link(dve.tensor_scalar(half_gap[:, :], half_gap[:, :], 0.5, None, ALU.mult))
                dve.tensor_scalar(spread[:, :], spread[:, :], 1.0 / D, LN_EPS, ALU.mult, ALU.add).then_inc(dve_step, 1)
                done.next()
                link(dve.tensor_tensor(half_gap[:, :], half_gap[:, :], half_gap[:, :], ALU.mult))
                return dve.tensor_tensor(var_eps[:, :], spread[:, :], half_gap[:, :], ALU.add)

            def per_row_sum(i, g):
                dve.wait_ge(exped, i * GROUPS + (g + 1))
                dve.reciprocal(per_sum[:, g % 2], row_sum[:, g % 2]).then_inc(sums_ready, 1)

            def peak_of_x2(i):
                dve.wait_ge(xn2_ready, i)
                link(dve.tensor_reduce(xn2_peak[:, :], xn2[:, :, :], AX.XY, ALU.max, apply_absolute_value=True))
                link(dve.tensor_tensor(keep["x2_peak"][:, :], keep["x2_peak"][:, :], xn2_peak[:, :], ALU.max))

            def rotate(g, b, n):
                src = raw[:, g % 2]
                sin = keep["sin"][:, :].unsqueeze(1).to_broadcast([P, 2, SEQ])
                cos = keep["cos"][:, :].unsqueeze(1).to_broadcast([P, 2, SEQ])
                dve.wait_ge(emptied[b], n + 1)
                link(dve.tensor_tensor(by_sin[:, :, :], src, sin, ALU.mult))
                dve.tensor_tensor(by_cos[:, :, :], src, cos, ALU.mult).then_inc(raw_used, 1)
                dve.stream_shuffle(sin_turned[:, :, :].rearrange("p a t -> p (a t)"),
                                   by_sin[:, :, :].rearrange("p a t -> p (a t)"), HALF_TURN).then_inc(dve_step, 1)
                dve.wait_ge(dve_step, done.next())
                dve.tensor_tensor(qk[:, g], by_cos[:, :, :], sin_turned[:, :, :], ALU.add).then_inc(rotated, 1)

            def turn(i, steps, par):
                names = [s for s, _ in steps]
                if steps[0][0] == "matrix":
                    link(dve.tensor_copy(inv_now[:, :], keep["inv"][:, bass.ds(steps[0][1] + MG, 1)]))
                late = []
                if "scores" in names and "out" in names:
                    late.append((rotate, (GROUPS - 1, *ring.back(2))))
                waiting, last_job = False, None
                for s, g in steps:
                    if waiting and s != "turn_p":
                        for f, args in late:
                            f(*args)
                        late, waiting = [], False
                        if last_job:
                            last_job[0](*last_job[1])
                            last_job = None
                    if s == "quantise":
                        w = w_raw[:, g, :].rearrange("p (k j) -> p k j", j=QBLOCK)
                        q = w_deq[:, g, :].rearrange("p (k j) -> p k j", j=QBLOCK)
                        st = step[:, g, :]
                        dve.wait_ge(w_in[g], i * 16)
                        link(dve.tensor_reduce(block_max[:, :], w, AX.X, ALU.max, apply_absolute_value=True))
                        link(dve.tensor_scalar(st, block_max[:, :], 1.0 / WMAX, STEP_FLOOR, ALU.mult, ALU.max))
                        link(dve.reciprocal(per_step[:, :], st))
                        link(dve.tensor_tensor(q, w, per_step[:, :].unsqueeze(2).to_broadcast([P, D // QBLOCK, QBLOCK]),
                                               ALU.mult))
                        link(dve.tensor_scalar(q, q, MAGIC, MAGIC + WMAX, ALU.add, ALU.min))
                        link(dve.tensor_scalar(st, st, inv_now[:, :], None, ALU.mult))
                        dve.tensor_scalar(q, q, MAGIC - WMAX - 1.0, MAGIC, ALU.max, ALU.subtract).then_inc(w_rounded, 1)
                    if s == "weight":
                        b, n = ring.next()
                        dve.wait_ge(w_hi, (i - 1) * UNITS + (g + 1))
                        dve.tensor_tensor(parts[:, g, 1].rearrange("p c o -> p (c o)"), banks[:, b, :],
                                          parts[:, g, 0].rearrange("p c o -> p (c o)"), ALU.subtract).then_inc(emptied[b], 1)
                    if s == "norm":
                        dve.wait_ge(x_loaded, i * 16 + 48)
                        for t in range(TT):
                            ins = dve.bn_stats(stats[:, t, :], x_in[:, t, :])
                            if t == TT - 1:
                                link(ins)
                        mean_and_var(stats, mean, var_eps).then_inc(var_ready, 1)
                        dve.wait_ge(rstd_ready, i + 3)
                        for t in range(TT):
                            last = dve.tensor_scalar(xn[:, t, :], x_in[:, t, :], mean[:, t:t + 1], rstd[:, t:t + 1],
                                                     ALU.subtract, ALU.mult)
                        last.then_inc(xn_ready, 1)
                    if s == "turn":
                        for k in range(2 * TT):
                            b, n = ring.next()
                            dve.wait_ge(turn_hi, i * (2 * TT) + (2 * TT + k + 1))
                            t = k % TT
                            src = banks[:, b, :].rearrange("p (c o) -> p c o", c=DC)
                            if k < TT:
                                dve.tensor_tensor(xt[:, 1, :, t * P:(t + 1) * P], src, xt[:, 0, :, t * P:(t + 1) * P],
                                                  ALU.subtract).then_inc(emptied[b], 1)
                            else:
                                dve.scalar_tensor_tensor(
                                    out=ct[:, 1, :, t * P:(t + 1) * P], in0=src, scalar=keep["inv"][:, MC:MC + 1],
                                    in1=ct[:, 0, :, t * P:(t + 1) * P], op0=ALU.mult,
                                    op1=ALU.subtract).then_inc(emptied[b], 1)
                    if s == "value":
                        for _ in range(TT):
                            ring.next()
                    if s == "query_key":
                        b, n = ring.next()
                        if "scores" in names:
                            late.append((rotate, (g, b, n)))
                        else:
                            rotate(g, b, n)
                    if s == "scores":
                        dve.wait_ge(scored, i * GROUPS + (g + 1))
                        dve.tensor_reduce(neg_max[:, 0, :], score_banks[:, :, 0:P], AX.X, ALU.max,
                                          negate=True).then_inc(dve_step, 1)
                        done.next()
                        link(dve.tensor_reduce(neg_max[:, 1, :], score_banks[:, :, P:3 * P], AX.X, ALU.max, negate=True))
                        dve.tensor_scalar(neg_max[:, :, :], neg_max[:, :, :], SCORE_SCALE, None,
                                          ALU.mult).then_inc(max_ready, 1)
                        late.append((per_row_sum, (i, g)))
                        waiting = True
                    if s == "turn_p":
                        for _ in range(3):
                            ring.next()
                    if s == "apply":
                        ib = i - 1 if g == GROUPS - 1 else i
                        b, n = ring.next()
                        dve.wait_ge(heads_hi, ib * GROUPS + (g + 1))
                        dve.tensor_tensor(ot[:, 1, g, :], banks[:, b, 0:SEQ], ot[:, 0, g, :],
                                          ALU.subtract).then_inc(emptied[b], 1)
                    if s == "out":
                        if not isinstance(i, int) or i > 1:
                            dve.wait_ge(x2_stored, i * 16 - 16)
                        dve.wait_ge(xb_ready, i)
                        for t in range(TT):
                            b, n = ring.next()
                            dve.wait_ge(filled[b], n)
                            dve.scalar_tensor_tensor(out=x2[:, t, :], in0=banks[:, b, :], scalar=keep["back"][:, 2:3],
                                                     in1=xb[:, t, :], op0=ALU.mult, op1=ALU.add).then_inc(emptied[b], 1)
                            dve.wait_ge(emptied[b], n + 1)
                            dve.bn_stats(stats2[:, t, :], x2[:, t, :]).then_inc(x2_ready, 1)
                        dve.wait_ge(x2_ready, i * TT)
                        mean_and_var(stats2, mean2, var_eps2).then_inc(var2_ready, 1)
                        dve.wait_ge(rstd2_ready, i)
                        for t in range(TT):
                            last = dve.tensor_scalar(xn2[:, t, :], x2[:, t, :], mean2[:, t:t + 1], rstd2[:, t:t + 1],
                                                     ALU.subtract, ALU.mult)
                        last.then_inc(xn2_ready, 1)
                        last_job = (peak_of_x2, (i,))
                    if s == "turn_x2":
                        for _ in range(TT):
                            ring.next()
                if last_job:
                    last_job[0](*last_job[1])

            links = 1 + 7 + GROUPS * 2 + GROUPS * 2 + 7 + 2 + UNITS * 6
            turns(dve, turn, [(f, FILLS, RING) for f in ring.fills] + [(done, BODY * links + 1, BODY)])

        @block.scalar
        def _(act):
            ring = Ring(RING)
            for b in range(RING):
                act.sem_inc(emptied[b], 1)
            act.sem_inc(raw_used, 2)
            act.sem_inc(w_quantised, UNITS)
            for k in range(UNITS):
                act.sem_inc(parts_stored[k], 16)

            def exps(i, g):
                act.wait_ge(max_ready, i * GROUPS + (g + 1))
                for h in range(HG):
                    for part, (lo, hi) in enumerate(((0, P), (P, 3 * P))):
                        last = act.activation(prob[:, g % 2, h, lo:hi], score_banks[:, h, lo:hi], ACT.Exp,
                                              bias=neg_max[:, part, h:h + 1], scale=SCORE_SCALE,
                                              accum_out=row_sum[:, g % 2, part, h:h + 1])
                last.then_inc(exped, 1)

            def turn(i, steps, par):
                pending = None
                for s, g in steps:
                    if pending is not None and s != "turn_p":
                        exps(*pending)
                        pending = None
                    if s == "turn":
                        for k in range(2 * TT):
                            b, n = ring.next()
                            t = k % TT
                            src = banks[:, b, :].rearrange("p (c o) -> p c o", c=DC)
                            act.wait_ge(filled[b], n)
                            if k < TT:
                                act.activation(xt[:, 0, :, t * P:(t + 1) * P], src, ACT.Copy).then_inc(turn_hi, 1)
                            else:
                                act.activation(ct[:, 0, :, t * P:(t + 1) * P], src, ACT.Copy,
                                               scale=keep["inv"][:, MC:MC + 1]).then_inc(turn_hi, 1)
                    if s == "value":
                        for t in range(TT):
                            b, n = ring.next()
                            act.wait_ge(filled[b], n)
                            act.activation(v[:, par, t, :], banks[:, b, :], ACT.Copy).then_inc(emptied[b], 1)
                    if s == "weight":
                        b, n = ring.next()
                        act.wait_ge(filled[b], n)
                        act.wait_ge(parts_stored[g], i * 16)
                        act.activation(parts[:, g, 0].rearrange("p c o -> p (c o)"), banks[:, b, :],
                                       ACT.Copy).then_inc(w_hi, 1)
                    if s == "query_key":
                        b, n = ring.next()
                        act.wait_ge(filled[b], n)
                        act.wait_ge(raw_used, i * GROUPS + (GROUPS + g + 1))
                        act.activation(raw[:, g % 2, 0, :], banks[:, b, 0:SEQ], ACT.Identity,
                                       bias=keep["bqk"][:, g:g + 1], scale=keep["back"][:, 0:1])
                        act.activation(raw[:, g % 2, 1, :], banks[:, b, SEQ:2 * SEQ], ACT.Identity,
                                       bias=keep["bqk"][:, DC + g:DC + g + 1],
                                       scale=keep["back"][:, 1:2]).then_inc(emptied[b], 1)
                    if s == "scores":
                        pending = (i, g)
                    if s == "turn_p":
                        for half in range(2):
                            b, n = ring.next()
                            act.wait_ge(filled[b], n)
                            act.activation(pt0[:, 2 * half:2 * half + 2, :],
                                           banks[:, b, :].rearrange("p (h q) -> p h q", h=2),
                                           ACT.Copy).then_inc(emptied[b], 1)
                        b, n = ring.next()
                        act.wait_ge(filled[b], n)
                        act.activation(pt1[:, :, :], banks[:, b, :].rearrange("p (h q) -> p h q", h=HG),
                                       ACT.Copy).then_inc(emptied[b], 1)
                        if pending is not None:
                            exps(*pending)
                            pending = None
                    if s == "apply":
                        b, n = ring.next()
                        act.wait_ge(filled[b], n)
                        act.activation(ot[:, 0, g, :], banks[:, b, 0:SEQ], ACT.Copy).then_inc(heads_hi, 1)
                    if s == "out":
                        for _ in range(TT):
                            ring.next()
                    if s == "turn_x2":
                        if not isinstance(i, int) or i > 1:
                            act.wait_ge(xt2_stored, i * 16 - 16)
                        for t in range(TT):
                            b, n = ring.next()
                            act.wait_ge(filled[b], n)
                            act.activation(xt2[:, :, t * P:(t + 1) * P],
                                           banks[:, b, :].rearrange("p (c o) -> p c o", c=DC),
                                           ACT.Copy).then_inc(emptied[b], 1)
                if pending is not None:
                    exps(*pending)

            turns(act, turn, [(f, FILLS, RING) for f in ring.fills])

        @block.tensor
        def _(pe):
            ring = Ring(RING)
            attn_hi, attn_lo, ident = keep["attn_hi"], keep["attn_lo"], keep["ident"]

            def fill():
                b, n = ring.next()
                pe.wait_ge(emptied[b], n)
                return b, n

            def three(out, pairs):
                count = 3 * len(pairs)
                k = 0
                for (w_hi, w_lo), (m_hi, m_lo) in pairs:
                    for w, m in ((w_hi, m_hi), (w_hi, m_lo), (w_lo, m_hi)):
                        last = pe.matmul(out, w, m, start=(k == 0), stop=(k == count - 1))
                        k += 1
                return last

            def turn(i, steps, par):
                for s, g in steps:
                    if s == "turn":
                        for k in range(2 * TT):
                            b, n = fill()
                            if k == 0:
                                pe.wait_ge(xn_ready, i + 2)
                            if k == TT:
                                pe.wait_ge(c_loaded, i * 16 + 32)
                            src = xn if k < TT else c_in
                            for c in range(DC):
                                last = pe.transpose(banks[:, b, c * P:(c + 1) * P], src[:, k % TT, c * P:(c + 1) * P],
                                                    ident[:, :])
                            last.then_inc(filled[b], 1)
                            turned = (b, n + 1)
                    if s == "value":
                        for t in range(TT):
                            b, n = fill()
                            tile = slice(t * P, (t + 1) * P)
                            three(banks[:, b, :], [((ct[:, 0, c, tile], ct[:, 1, c, tile]),
                                                    (attn_hi[:, MV, c, :], attn_lo[:, MV, c, :]))
                                                   for c in range(DC)]).then_inc(filled[b], 1)
                            v_out = (b, n + 1)
                    if s == "weight":
                        b, n = fill()
                        pe.wait_ge(w_quantised, (i - 1) * UNITS + (UNITS + g + 1))
                        for c in range(DC):
                            last = pe.transpose(banks[:, b, c * P:(c + 1) * P], w_deq[:, g, c * P:(c + 1) * P], ident[:, :])
                        last.then_inc(filled[b], 1)
                    if s == "query_key":
                        if g == 0:
                            pe.wait_ge(emptied[turned[0]], turned[1])
                        b, n = fill()
                        cols = slice(g * P, (g + 1) * P)
                        for m, src in ((MQ, xt), (MK, ct)):
                            last = three(banks[:, b, m * SEQ:(m + 1) * SEQ],
                                         [((attn_hi[:, m, c, cols], attn_lo[:, m, c, cols]),
                                           (src[:, 0, c, :], src[:, 1, c, :])) for c in range(DC)])
                        last.then_inc(filled[b], 1)
                    if s == "scores":
                        pe.wait_ge(rotated, i * GROUPS + (g + 1))
                        if g > 0 or not isinstance(i, int) or i > 0:
                            pe.wait_ge(exped, i * GROUPS + g)
                        for h in range(HG):
                            f = slice(h * HD, (h + 1) * HD)
                            pe.matmul(score_banks[:, h, 0:P], qk[f, g, 0, 0:P], qk[f, g, 1, 0:P], start=True, stop=False)
                        for h in range(HG):
                            f = slice(h * HD, (h + 1) * HD)
                            pe.matmul(score_banks[:, h, P:3 * P], qk[f, g, 0, P:2 * P], qk[f, g, 1, :],
                                      start=False, stop=False)
                        for h in range(HG):
                            last = pe.matmul(score_banks[:, h, :].rearrange("p (a c) -> p a c", c=2 * P)[:, :, 0:P],
                                             keep["ident_b"][:, :], keep["mask"][:, :], start=False, stop=True)
                        last.then_inc(scored, 1)
                    if s == "turn_p":
                        ib = i - 1 if g == GROUPS - 1 else i
                        pe.wait_ge(normed, ib * GROUPS + (g + 1))
                        outs = []
                        for half in range(2):
                            b, n = fill()
                            for h in range(2):
                                for q in range(TT):
                                    last = pe.transpose(banks[:, b, h * SEQ + q * P:h * SEQ + (q + 1) * P],
                                                        prob[:, g % 2, 2 * half + h, q * P:(q + 1) * P], ident[:, :])
                            last.then_inc(filled[b], 1)
                            outs.append((b, n + 1))
                        b, n = fill()
                        for h in range(HG):
                            last = pe.transpose(banks[:, b, h * P:(h + 1) * P], prob[:, g % 2, h, 2 * P:3 * P], ident[:, :])
                        last.then_inc(filled[b], 1)
                        outs.append((b, n + 1))
                    if s == "apply":
                        vp = v[:, 1 - par if g == GROUPS - 1 else par]
                        b, n = fill()
                        for k, n_out in outs:
                            pe.wait_ge(emptied[k], n_out)
                        for h in range(HG):
                            cols = slice((g * HG + h) * HD, (g * HG + h + 1) * HD)
                            pe.matmul(banks[h * HD:(h + 1) * HD, b, 0:SEQ], vp[:, 0, cols], pt0[:, h, :],
                                      start=True, stop=False)
                        for h in range(HG):
                            cols = slice((g * HG + h) * HD, (g * HG + h + 1) * HD)
                            last = pe.matmul(banks[h * HD:(h + 1) * HD, b, P:SEQ], vp[:, 1, cols], pt1[:, h, :],
                                             start=False, stop=True)
                        last.then_inc(filled[b], 1)
                        heads_out = (b, n + 1)
                    if s == "out":
                        pe.wait_ge(emptied[heads_out[0]], heads_out[1])
                        for t in range(TT):
                            b, n = fill()
                            tile = slice(t * P, (t + 1) * P)
                            three(banks[:, b, :], [((ot[:, 0, c, tile], ot[:, 1, c, tile]),
                                                    (attn_hi[:, MO, c, :], attn_lo[:, MO, c, :]))
                                                   for c in range(DC)]).then_inc(filled[b], 1)
                    if s == "turn_x2":
                        pe.wait_ge(xn2_ready, i)
                        for t in range(TT):
                            b, n = fill()
                            for c in range(DC):
                                last = pe.transpose(banks[:, b, c * P:(c + 1) * P], xn2[:, t, c * P:(c + 1) * P], ident[:, :])
                            last.then_inc(filled[b], 1)

            turns(pe, turn, [(f, FILLS, RING) for f in ring.fills])


N = 512
TOK = BATCH * SEQ
NG = TOK // N
W2 = 2 * N
PIECES = TOK // W2


def hold(eng, sem, value, held):
    eng.wait_ge(sem, value)
    eng.sem_inc(held, 1)


class Scales:
    names = ("top", "x_step", "x_per", "g_step", "g_per", "a_step", "a_per", "a_unit", "a_fold",
             "u_step", "u_per", "o_step", "o_per", "o_unit", "o_fold", "g_back", "u_back", "d_back")

    def __init__(self, tile):
        self.tile = tile

    def __getitem__(self, name):
        k = self.names.index(name)
        return self.tile[:, k:k + 1]


def quantum(dve, link, sc, what, unit=None):
    if unit is not None:
        link(dve.tensor_tensor(sc["top"], sc["top"], unit, ALU.mult))
    link(dve.tensor_scalar(sc[what + "_step"], sc["top"], 1.0 / QMAX, STEP_FLOOR, ALU.mult, ALU.max))
    link(dve.reciprocal(sc[what + "_per"], sc[what + "_step"]))


def project(nc, io, keep, sc, xq, qg, phase):
    up = phase == "up"
    turns_of_2 = IC // 2
    with ExitStack() as ctx:
        def buf(name, shape, dt):
            return ctx.enter_context(nc.sbuf_tensor(f"{phase}_{name}", shape, dt))

        def sem(name):
            return ctx.enter_context(nc.semaphore(f"{phase}_{name}"))

        ST, CB = 2, 4
        w = buf("w", [P, 2, 2, DC, P], F16)
        stage = buf("stage", [P, ST, W2], F32)
        peaks = buf("peaks", [P, 2 * PIECES], F32)
        if up:
            chain = buf("chain", [P, CB, W2], F32)
            sig_steps = buf("sig_steps", [P, 2, W2], U16)
            size = buf("size", [P, CB // 2, W2], I16)
            act_peaks = buf("act_peaks", [P, 4 * PIECES], F32)
        else:
            xt_in = buf("xt_in", [P, 2, DC, N], F32)
            x_steps = buf("x_steps", [P, DC, N], I16)
        banks = ctx.enter_context(nc.psum_tensor(f"{phase}_banks", [P, 4, 2, N], F32))

        w_in = [sem(f"w_in{b}") for b in range(2)]
        xt_loaded = [sem(f"xt_loaded{b}") for b in range(2)]
        xq_ready = sem("xq_ready")
        filled, staged, peaked = sem("filled"), sem("staged"), sem("peaked")
        stored = [sem(f"stored{b}") for b in range(ST)]
        joined, top_ready, scales_ready = sem("joined"), sem("top_ready"), sem("scales_ready")
        joined2, top2_ready, scales2_ready = sem("joined2"), sem("top2_ready"), sem("scales2_ready")
        chain_in = [sem(f"chain_in{b}") for b in range(CB)]
        steps_ready, sig_ready, act_done, act_steps = sem("steps_ready"), sem("sig_ready"), sem("act_done"), sem("act_steps")
        dve_step, held_act, held_dve = sem("dve_step"), sem("held_act"), sem("held_dve")
        block = ctx.enter_context(nc.Block())

        dst = (io["ups"] if up else io["gates"]).rearrange("m p (j c) -> m p j c", c=W2)
        gates = io["gates"].rearrange("(k a) p (j c) -> k p a j c", c=W2, a=4)
        w_units = io["w_parts"][IC:2 * IC] if up else io["w_parts"][0:IC]
        run_peak = keep["run_peak"]
        act_run = keep["act_peak"]

        @block.sync
        def _(sp):
            for b in range(2):
                sp.dma_start(w[:, b], w_units[b]).then_inc(w_in[b], 16)
            if not up:
                for n in range(NG):
                    if n >= 2:
                        sp.wait_ge(xq_ready, n - 1)
                    for j in range(N // SEQ):
                        sp.dma_start(xt_in[:, n % 2, :, j * SEQ:(j + 1) * SEQ],
                                     io["xt2"][n * (N // SEQ) + j]).then_inc(xt_loaded[n % 2], 16)
            piece = Tally()
            fills = Tally()

            def weights(i, b):
                sp.wait_ge(filled, fills.value)
                sp.dma_start(w[:, b], row(w_units, i * 2 + (2 + b))).then_inc(w_in[b], 16)

            acts = Tally()
            n_chain = 4 * PIECES

            def turn(i, second, more, chain_first):
                c = 0
                for a in range(2):
                    for j in range(PIECES):
                        if up and not second:
                            for _ in range(2):
                                if chain_first and c < CB:
                                    pass
                                else:
                                    sp.wait_ge(act_done, acts.next())
                                q, r = divmod(c, PIECES)
                                g = row(gates, i)[:, q, r, :]
                                sp.dma_start(chain[:, c % CB, :], g).then_inc(chain_in[c % CB], 16)
                                c += 1
                        sp.wait_ge(staged, piece.next())
                        sp.dma_start(row(dst, i * 2 + a)[:, j, :], stage[:, j % ST, :]).then_inc(stored[j % ST], 16)
                    fills.value = fills.value + PIECES
                    fills.made += 1
                    if more:
                        weights(i, a)

            half_way = turns_of_2 // 2
            if up:
                turn(0, False, True, True)
                with loop(sp, 1, half_way, [(piece, 2 * PIECES), (acts, n_chain)]) as i:
                    fills.value = i * (2 * PIECES)
                    turn(i, False, True, False)
                with loop(sp, half_way, turns_of_2 - 1, [(piece, 2 * PIECES)]) as i:
                    fills.value = i * (2 * PIECES)
                    turn(i, True, True, False)
            else:
                with loop(sp, 0, turns_of_2 - 1, [(piece, 2 * PIECES)]) as i:
                    fills.value = i * (2 * PIECES)
                    turn(i, True, True, False)
            turn(turns_of_2 - 1, True, False, False)
            for b in range(ST):
                sp.wait_ge(stored[b], 16 * (IC * PIECES // ST + 1))

        @block.tensor
        def _(pe):
            weights_in = [Tally(by=16), Tally(by=16)]
            emptied = Tally(-4)

            def turn(i, first):
                for a in range(2):
                    pe.wait_ge(w_in[a], weights_in[a].next())
                    for j in range(PIECES):
                        if first and a == 0:
                            if not up:
                                pe.wait_ge(xq_ready, 2 * j + 1)
                            emptied.next()
                        else:
                            pe.wait_ge(staged, emptied.next())
                        for half in range(2):
                            n = 2 * j + half
                            if first and a == 0 and half and not up:
                                pe.wait_ge(xq_ready, n + 1)
                            k = 0
                            for c in range(DC):
                                for wp, xp in ((0, 0), (0, 1), (1, 0)):
                                    last = pe.matmul(banks[:, j, half, :], w[:, a, wp, c, :], xq[:, xp, n, c, :],
                                                     start=(k == 0), stop=(k == 3 * DC - 1))
                                    k += 1
                        last.then_inc(filled, 1)

            turn(0, True)
            with loop(pe, 1, turns_of_2, [(weights_in[0], 1), (weights_in[1], 1), (emptied, 2 * PIECES)]) as i:
                turn(i, False)

        @block.scalar
        def _(act):
            for b in range(ST):
                act.sem_inc(stored[b], 16)
            act.sem_inc(peaked, ST)
            back = sc["u_back"] if up else sc["g_back"]
            fills, free = Tally(), Tally()
            store = [Tally(by=16) for _ in range(ST)]
            act.wait_ge(scales_ready, 1)

            def evacuate(j):
                act.wait_ge(filled, fills.next())
                act.wait_ge(peaked, free.next())
                act.wait_ge(stored[j % ST], store[j % ST].next())
                act.activation(stage[:, j % ST, :], banks[:, j].rearrange("p h n -> p (h n)"), ACT.Copy,
                               scale=back).then_inc(staged, 1)

            per_turn = [(fills, 2 * PIECES), (free, 2 * PIECES)] + [(t, 2 * PIECES // ST) for t in store]
            if not up:
                with loop(act, 0, turns_of_2, per_turn):
                    for a in range(2):
                        for j in range(PIECES):
                            evacuate(j)
                return

            loads = [Tally(by=16) for _ in range(CB)]
            steps = Tally()

            def piece_of(k, c):
                q, r = divmod(c, PIECES)
                start = k * (4 * TOK) + (q * TOK + r * W2)
                return qg[:, bass.ds(start, W2)]

            half_way = turns_of_2 // 2
            n_chain = 4 * PIECES
            with loop(act, 0, half_way, per_turn + [(t, n_chain // CB) for t in loads] + [(steps, n_chain)]) as i:
                c = 0
                for a in range(2):
                    for j in range(PIECES):
                        evacuate(j)
                        for _ in range(2):
                            b = c % CB
                            hold(act, chain_in[b], loads[b].next(), held_act)
                            if c % 2 == 0:
                                act.activation(size[:, c % CB // 2, :], chain[:, b, :], ACT.Abs, scale=sc["g_per"])
                            act.activation(piece_of(i, c), chain[:, b, :], ACT.Copy, scale=sc["g_per"]).then_inc(steps_ready, 1)
                            hold(act, steps_ready, steps.next(), held_act)
                            act.activation(chain[:, b, :], piece_of(i, c), ACT.Sigmoid,
                                           scale=sc["g_step"]).then_inc(sig_ready, 1)
                            c += 1
            act.wait_ge(scales2_ready, 1)
            act.sem_inc(act_steps, 1)
            done2 = Tally(IC * PIECES)

            def steps_of(k, c):
                hold(act, act_done, done2.next(), held_act)
                act.activation(piece_of(k, c), chain[:, c % CB, :], ACT.Copy, scale=sc["a_fold"]).then_inc(act_steps, 1)

            with loop(act, 0, half_way, per_turn + [(done2, n_chain)]) as i:
                c = 0
                for a in range(2):
                    for j in range(PIECES):
                        evacuate(j)
                        for _ in range(2):
                            act.activation(chain[:, c % CB, :], piece_of(i, c), ACT.Sigmoid,
                                           scale=sc["g_step"]).then_inc(sig_ready, 1)
                            if c > 0:
                                steps_of(i, c - 1)
                            c += 1
                steps_of(i, c - 1)

        @block.gpsimd
        def _(pool):
            pool.wait_ge(joined, 1)
            pool.partition_all_reduce(sc["top"], run_peak[:, 0:1], P, REDUCE.max).then_inc(top_ready, 1)
            if up:
                pool.wait_ge(joined2, 1)
                pool.partition_all_reduce(sc["top"], act_run[:, 0:1], P, REDUCE.max).then_inc(top2_ready, 1)

        @block.vector
        def _(dve):
            done = Tally()

            def link(ins):
                ins.then_inc(dve_step, 1)
                dve.wait_ge(dve_step, done.next())

            pieces = Tally()
            if not up:
                dve.tensor_copy(run_peak[:, 0:1], keep["x2_peak"][:, :]).then_inc(joined, 1)
                dve.wait_ge(top_ready, 1)
                quantum(dve, link, sc, "x")
                link(dve.tensor_tensor(sc["g_back"], sc["x_step"], keep["half"][:, MG:MG + 1], ALU.mult))
                link(dve.memset(run_peak[:, :], 0.0))
                dve.tensor_tensor(sc["u_back"], sc["x_step"], keep["half"][:, MU:MU + 1], ALU.mult).then_inc(scales_ready, 1)
                for n in range(NG):
                    dve.wait_ge(xt_loaded[n % 2], 16 * (N // SEQ) * (n // 2 + 1))
                    if n > 0:
                        dve.wait_ge(xq_ready, n)
                    link(dve.tensor_scalar(x_steps[:, :, :], xt_in[:, n % 2], sc["x_per"], None, ALU.mult))
                    link(dve.tensor_copy(xq[:, 0, n], x_steps[:, :, :]))
                    dve.tensor_tensor(xq[:, 1, n], x_steps[:, :, :], xq[:, 0, n], ALU.subtract).then_inc(xq_ready, 1)
            else:
                link(dve.tensor_reduce(run_peak[:, 0:1], run_peak[:, :], AX.X, ALU.max))
                link(dve.memset(act_run[:, :], 0.0))
                dve.tensor_copy(act_run[:, 0:1], act_run[:, 0:1]).then_inc(joined, 1)
                dve.wait_ge(top_ready, 1)
                link(dve.memset(run_peak[:, :], 0.0))
                quantum(dve, link, sc, "g")
                dve.tensor_scalar(sc["a_unit"], sc["g_step"], 1.0 / SIG, None, ALU.mult).then_inc(scales_ready, 1)
                dve.wait_ge(scales_ready, 1)

            def peak_of(a, j):
                dve.wait_ge(staged, pieces.next())
                dve.tensor_reduce(peaks[:, a * PIECES + j:a * PIECES + j + 1], stage[:, j % ST, :], AX.X, ALU.max,
                                  apply_absolute_value=True).then_inc(peaked, 1)

            all_peaks = Tally(ST)

            def join():
                for _ in range(2 * PIECES):
                    all_peaks.next()
                dve.wait_ge(peaked, all_peaks.value)
                link(dve.tensor_tensor(run_peak[:, :], run_peak[:, :], peaks[:, :], ALU.max))

            per_turn = [(pieces, 2 * PIECES), (all_peaks, 2 * PIECES)]
            if not up:
                with loop(dve, 0, turns_of_2, per_turn + [(done, 1)]):
                    for a in range(2):
                        for j in range(PIECES):
                            peak_of(a, j)
                    join()
                return

            sigs, acts = Tally(), Tally()

            def piece_of(k, c):
                q, r = divmod(c, PIECES)
                return qg[:, bass.ds(k * (4 * TOK) + (q * TOK + r * W2), W2)]

            half_way = turns_of_2 // 2
            n_chain = 4 * PIECES
            with loop(dve, 0, half_way, per_turn + [(done, n_chain + n_chain // 2 + 2), (sigs, n_chain), (acts, n_chain)]) as i:
                c = 0
                for a in range(2):
                    for j in range(PIECES):
                        peak_of(a, j)
                        for _ in range(2):
                            b = c % CB
                            dve.wait_ge(sig_ready, sigs.next())
                            link(dve.tensor_scalar(sig_steps[:, c % 2, :], chain[:, b, :], SIG, SIG - 1.0, ALU.mult, ALU.min))
                            if c % 2 == 0:
                                dve.sem_inc(held_dve, 1)
                                dve.tensor_tensor_reduce(out=chain[:, b, :], in0=size[:, c % CB // 2, :],
                                                         in1=sig_steps[:, c % 2, :], scale=1.0, scalar=0.0, op0=ALU.mult,
                                                         op1=ALU.max, accum_out=act_peaks[:, c:c + 1]).then_inc(act_done, 1)
                            else:
                                link(dve.tensor_tensor(chain[:, b, :], piece_of(i, c), sig_steps[:, c % 2, :], ALU.mult))
                                dve.tensor_reduce(act_peaks[:, c:c + 1], chain[:, b, :], AX.X, ALU.max,
                                                  apply_absolute_value=True).then_inc(act_done, 1)
                            acts.next()
                            c += 1
                dve.wait_ge(act_done, acts.value)
                link(dve.tensor_tensor(act_run[:, :], act_run[:, :], act_peaks[:, :], ALU.max))
                join()
            link(dve.tensor_reduce(act_run[:, 0:1], act_run[:, :], AX.X, ALU.max))
            dve.tensor_copy(act_run[:, 1:2], act_run[:, 0:1]).then_inc(joined2, 1)
            dve.wait_ge(top2_ready, 1)
            quantum(dve, link, sc, "a", unit=sc["a_unit"])
            dve.tensor_tensor(sc["a_fold"], sc["a_unit"], sc["a_per"], ALU.mult).then_inc(scales2_ready, 1)
            written = Tally(IC * PIECES)
            with loop(dve, 0, half_way, per_turn + [(done, n_chain + 1), (sigs, n_chain), (written, n_chain)]) as i:
                c = 0
                for a in range(2):
                    for j in range(PIECES):
                        peak_of(a, j)
                        for _ in range(2):
                            b = c % CB
                            dve.wait_ge(act_done, written.value)
                            dve.wait_ge(sig_ready, sigs.next())
                            link(dve.tensor_scalar(sig_steps[:, c % 2, :], chain[:, b, :], SIG, SIG - 1.0, ALU.mult, ALU.min))
                            written.next()
                            dve.tensor_tensor(chain[:, b, :], piece_of(i, c), sig_steps[:, c % 2, :],
                                              ALU.mult).then_inc(act_done, 1)
                            c += 1
                join()


def find_product_peak(nc, io, keep, sc, qg):
    CB = 4
    with ExitStack() as ctx:
        def buf(name, shape, dt):
            return ctx.enter_context(nc.sbuf_tensor("peak_" + name, shape, dt))

        def sem(name):
            return ctx.enter_context(nc.semaphore("peak_" + name))

        u = buf("u", [P, CB, W2], F32)
        u_steps = buf("u_steps", [P, PIECES, W2], I16)
        a_size = buf("a_size", [P, PIECES // 2, W2], I16)
        product = buf("product", [P, 2, W2], F32)
        peaks = buf("peaks", [P, 2 * PIECES], F32)
        u_in = [sem(f"u_in{b}") for b in range(CB)]
        joined, top_ready, scales_ready = sem("joined"), sem("top_ready"), sem("scales_ready")
        steps_ready, steps_used = sem("steps_ready"), sem("steps_used")
        joined2, top2_ready = sem("joined2"), sem("top2_ready")
        dve_step, held = sem("dve_step"), sem("held")
        block = ctx.enter_context(nc.Block())
        ups = io["ups"].rearrange("m p (j c) -> m p j c", c=W2)
        run_peak = keep["run_peak"]

        @block.sync
        def _(sp):
            used = Tally()

            def load_w_down(m):
                dst = keep["w_down"][:, bass.ds(m, 1)].rearrange("p z a c o -> p (z a) c o")
                sp.dma_start(dst, row(io["w_parts"], m + 2 * IC)).then_inc(keep["w_down_in"], 16)

            for j in range(PIECES):
                sp.dma_start(u[:, j, :], ups[0][:, j, :]).then_inc(u_in[j], 16)
            with loop(sp, 1, IC, [(used, PIECES)]) as m:
                load_w_down(m - 1)
                for j in range(PIECES):
                    sp.wait_ge(steps_ready, used.next())
                    sp.dma_start(u[:, j, :], row(ups, m)[:, j, :]).then_inc(u_in[j], 16)
            load_w_down(IC - 1)
            sp.wait_ge(keep["w_down_in"], 16 * IC)

        @block.scalar
        def _(act):
            act.sem_inc(steps_used, PIECES)
            act.wait_ge(scales_ready, 1)
            loads, free = [Tally(by=16) for _ in range(CB)], Tally()
            with loop(act, 0, IC, [(t, 1) for t in loads] + [(free, PIECES)]) as m:
                for j in range(PIECES):
                    act.wait_ge(u_in[j], loads[j].next())
                    act.wait_ge(steps_used, free.next())
                    if j % 2:
                        act.activation(u_steps[:, j, :], u[:, j, :], ACT.Copy, scale=sc["u_per"]).then_inc(steps_ready, 1)
                    else:
                        act.activation(u_steps[:, j, :], u[:, j, :], ACT.Abs, scale=sc["u_per"])
                        act.activation(a_size[:, j // 2, :], qg[:, bass.ds(m * TOK + j * W2, W2)], ACT.Abs).then_inc(steps_ready, 1)

        @block.gpsimd
        def _(pool):
            pool.wait_ge(joined, 1)
            pool.partition_all_reduce(sc["top"], run_peak[:, 0:1], P, REDUCE.max).then_inc(top_ready, 1)
            pool.wait_ge(joined2, 1)
            pool.partition_all_reduce(sc["top"], run_peak[:, 0:1], P, REDUCE.max).then_inc(top2_ready, 1)

        @block.vector
        def _(dve):
            done = Tally()

            def link(ins):
                ins.then_inc(dve_step, 1)
                dve.wait_ge(dve_step, done.next())

            link(dve.tensor_reduce(run_peak[:, 0:1], run_peak[:, :], AX.X, ALU.max))
            dve.tensor_copy(run_peak[:, 1:2], run_peak[:, 0:1]).then_inc(joined, 1)
            dve.wait_ge(top_ready, 1)
            link(dve.memset(run_peak[:, :], 0.0))
            quantum(dve, link, sc, "u")
            dve.tensor_tensor(sc["o_unit"], sc["a_step"], sc["u_step"], ALU.mult).then_inc(scales_ready, 1)
            ready = Tally()
            with loop(dve, 0, IC // 2, [(done, PIECES + 1), (ready, 2 * PIECES)]) as k:
                for c in range(2 * PIECES):
                    j = c % PIECES
                    steps = qg[:, bass.ds(k * (2 * TOK) + c * W2, W2)]
                    dve.wait_ge(steps_ready, ready.next())
                    dve.wait_ge(steps_used, ready.value + 2)
                    if j % 2:
                        link(dve.tensor_tensor(product[:, 1, :], steps, u_steps[:, j, :], ALU.mult))
                        dve.tensor_reduce(peaks[:, c:c + 1], product[:, 1, :], AX.X, ALU.max,
                                          apply_absolute_value=True).then_inc(steps_used, 1)
                    else:
                        dve.sem_inc(held, 1)
                        dve.tensor_tensor_reduce(out=product[:, 0, :], in0=a_size[:, j // 2, :], in1=u_steps[:, j, :],
                                                 scale=1.0, scalar=0.0, op0=ALU.mult, op1=ALU.max,
                                                 accum_out=peaks[:, c:c + 1]).then_inc(steps_used, 1)
                dve.wait_ge(steps_used, ready.value + PIECES)
                link(dve.tensor_tensor(run_peak[:, :], run_peak[:, :], peaks[:, :], ALU.max))
            link(dve.tensor_reduce(run_peak[:, 0:1], run_peak[:, :], AX.X, ALU.max))
            dve.tensor_copy(run_peak[:, 1:2], run_peak[:, 0:1]).then_inc(joined2, 1)
            dve.wait_ge(top2_ready, 1)
            quantum(dve, link, sc, "o", unit=sc["o_unit"])
            link(dve.tensor_tensor(sc["o_fold"], sc["o_unit"], sc["o_per"], ALU.mult))
            link(dve.tensor_tensor(sc["d_back"], sc["o_step"], keep["half"][:, MD:MD + 1], ALU.mult))


def project_down(nc, io, keep, sc, qg):
    PR = IC // 2
    UB = 3
    TG = N // P
    with ExitStack() as ctx:
        def buf(name, shape, dt):
            return ctx.enter_context(nc.sbuf_tensor("down_" + name, shape, dt))

        def sem(name):
            return ctx.enter_context(nc.semaphore("down_" + name))

        u = buf("u", [P, UB, 2, N], F32)
        u_steps = buf("u_steps", [P, 2, 2, N], I16)
        product = buf("product", [P, 2, 2, N], F32)
        o_steps = buf("o_steps", [P, 2, 2, N], I16)
        oq = buf("oq", [P, 2, 2, IC, N], F16)
        y = buf("y", [P, TG, D], F32)
        banks = ctx.enter_context(nc.psum_tensor("down_banks", [P, TG, D], F32))
        u_in = [sem(f"u_in{b}") for b in range(UB)]
        x2_loaded = [sem(f"x2_loaded{t}") for t in range(TG)]
        y_stored = [sem(f"y_stored{t}") for t in range(TG)]
        u_ready, multiplied, o_ready, split = sem("u_ready"), sem("multiplied"), sem("o_ready"), sem("split")
        filled, summed = sem("filled"), sem("summed")
        dve_step = sem("dve_step")
        block = ctx.enter_context(nc.Block())
        ups = io["ups"].rearrange("(q a) p (n c) -> n q p a c", a=2, c=N)
        x2_tiles = io["x2"].rearrange("b (t p) d -> (b t) p d", p=P)
        out_tiles = io["out"].rearrange("b (t p) d -> (b t) p d", p=P)
        w_down = keep["w_down"][:, :, :, :, :].rearrange("p (r k) a c o -> p a k c r o", k=IC // DC)
        products = qg[:, :].rearrange("p (m t) -> p m t", t=TOK)

        @block.sync
        def _(sp):
            used, outs = Tally(-UB), Tally()
            stores = [Tally(-16, by=16) for _ in range(TG)]

            def load_u(n, q, first):
                if first:
                    used.next()
                else:
                    sp.wait_ge(u_ready, used.next())
                sp.dma_start(u[:, q % UB], row(ups[:, q], n)).then_inc(u_in[q % UB], 16)

            def load_x2(n, t, first):
                if first:
                    stores[t].next()
                else:
                    sp.wait_ge(y_stored[t], stores[t].next())
                sp.dma_start(y[:, t, :], row(x2_tiles, n * TG + t)).then_inc(x2_loaded[t], 16)

            def store(n, t):
                sp.wait_ge(summed, outs.next())
                sp.dma_start(row(out_tiles, n * TG + t), y[:, t, :]).then_inc(y_stored[t], 16)

            def group(n, start, before, before2):
                for q in range(PR):
                    load_u(n, q, start == 0 and q < UB)
                    if q < 2 and before2:
                        store(n - 2, 2 + q)
                    if q in (2, 3) and before:
                        load_x2(n - 1, 2 * (q - 2), start == 1)
                        load_x2(n - 1, 2 * (q - 2) + 1, start == 1)
                    if q > 3 and before:
                        store(n - 1, q - 4)

            group(0, 0, False, False)
            group(1, 1, True, False)
            with loop(sp, 1, NG // 2, [(used, 2 * PR), (outs, 2 * TG)] + [(t, 2) for t in stores]) as k:
                group(k * 2, 2, True, True)
                group(k * 2 + 1, 3, True, True)
            for t in (2, 3):
                store(NG - 2, t)
            for t in range(TG):
                load_x2(NG - 1, t, False)
            for t in range(TG):
                store(NG - 1, t)
            for t in range(TG):
                sp.wait_ge(y_stored[t], 16 * NG)

        @block.scalar
        def _(act):
            loads = [Tally(by=16) for _ in range(UB)]
            free_u, made, free_o = Tally(-2), Tally(), Tally(-2)

            def u_of(q, first):
                b = q % UB
                act.wait_ge(u_in[b], loads[b].next())
                if first:
                    free_u.next()
                else:
                    act.wait_ge(multiplied, free_u.next())
                act.activation(u_steps[:, q % 2], u[:, b], ACT.Copy, scale=sc["u_per"]).then_inc(u_ready, 1)

            def o_of(q, first):
                act.wait_ge(multiplied, made.next())
                if first:
                    free_o.next()
                else:
                    act.wait_ge(split, free_o.next())
                act.activation(o_steps[:, q % 2], product[:, q % 2], ACT.Copy, scale=sc["o_fold"]).then_inc(o_ready, 1)

            def group(first):
                for q in range(PR):
                    u_of(q, first and q < 2)
                    if q > 0:
                        o_of(q - 1, first and q - 1 < 2)
                o_of(PR - 1, False)

            group(True)
            group(False)
            with loop(act, 1, NG // 2, [(t, 2 * PR // UB) for t in loads] + [(t, 2 * PR) for t in (free_u, made, free_o)]):
                group(False)
                group(False)

        @block.vector
        def _(dve):
            us, os, done = Tally(), Tally(), Tally()
            free_p = Tally(-2)
            fills, x2s = Tally(), [Tally(by=16) for _ in range(TG)]

            def link(ins):
                ins.then_inc(dve_step, 1)
                dve.wait_ge(dve_step, done.next())

            def multiply(n, q, first):
                dve.wait_ge(u_ready, us.next())
                if first:
                    free_p.next()
                else:
                    dve.wait_ge(o_ready, free_p.next())
                dve.tensor_tensor(product[:, q % 2], products[:, 2 * q:2 * q + 2, bass.ds(n * N, N)], u_steps[:, q % 2],
                                  ALU.mult).then_inc(multiplied, 1)

            def parts(par, q, free):
                dve.wait_ge(o_ready, os.next())
                if free is not None:
                    dve.wait_ge(filled, free)
                link(dve.tensor_copy(oq[:, par, 0, 2 * q:2 * q + 2, :], o_steps[:, q % 2]))
                dve.tensor_tensor(oq[:, par, 1, 2 * q:2 * q + 2, :], o_steps[:, q % 2], oq[:, par, 0, 2 * q:2 * q + 2, :],
                                  ALU.subtract).then_inc(split, 1)

            def add(t):
                dve.wait_ge(filled, fills.next())
                dve.wait_ge(x2_loaded[t], x2s[t].next())
                dve.scalar_tensor_tensor(out=y[:, t, :], in0=banks[:, t, :], scalar=sc["d_back"], in1=y[:, t, :],
                                         op0=ALU.mult, op1=ALU.add).then_inc(summed, 1)

            def group(n, par, first, before, before2, free):
                for q in range(PR):
                    multiply(n, q, first and q < 2)
                    if q == 0 and before2:
                        add(TG - 1)
                    if q > 0:
                        parts(par, q - 1, free if q == 1 else None)
                    if q > 2 and before:
                        add(q - 3)
                parts(par, PR - 1, None)

            group(0, 0, True, False, False, None)
            group(1, 1, False, True, False, None)
            with loop(dve, 1, NG // 2, [(done, 2 * PR), (us, 2 * PR), (os, 2 * PR), (free_p, 2 * PR), (fills, 2 * TG)]
                      + [(t, 2) for t in x2s]) as k:
                for par in range(2):
                    group(k * 2 + par, par, False, True, True, k * (2 * TG) + (par - 1) * TG)
            add(TG - 1)
            for t in range(TG):
                add(t)

        @block.tensor
        def _(pe):
            ready, sums = Tally(), Tally(-TG)

            def group(par, first):
                for _ in range(PR):
                    ready.next()
                for t in range(TG):
                    if t == 0:
                        pe.wait_ge(split, ready.value)
                    if first:
                        sums.next()
                    else:
                        pe.wait_ge(summed, sums.next())
                    k = 0
                    for m in range(IC):
                        wk, c = divmod(m, DC)
                        for op, wp in ((0, 0), (1, 0), (0, 1)):
                            last = pe.matmul(banks[:, t, :], oq[:, par, op, m, t * P:(t + 1) * P], w_down[:, wp, wk, c],
                                             start=(k == 0), stop=(k == 3 * IC - 1))
                            k += 1
                    last.then_inc(filled, 1)

            group(0, True)
            group(1, False)
            with loop(pe, 1, NG // 2, [(ready, 2 * PR), (sums, 2 * TG)]):
                group(0, False)
                group(1, False)


def feed_forward(nc, io, keep):
    with ExitStack() as ctx:
        def buf(name, shape, dt):
            return ctx.enter_context(nc.sbuf_tensor(name, shape, dt))

        sc = Scales(buf("ffn_scales", [P, len(Scales.names)], F32))
        keep["run_peak"] = buf("run_peak", [P, 2 * PIECES], F32)
        keep["act_peak"] = buf("act_peak", [P, 4 * PIECES], F32)
        keep["w_down_in"] = ctx.enter_context(nc.semaphore("w_down_in"))
        qg = buf("qg", [P, IC * TOK], I16)
        with ExitStack() as wide:
            xq = wide.enter_context(nc.sbuf_tensor("xq", [P, 2, NG, DC, N], F16))
            project(nc, io, keep, sc, xq, qg, "gate")
            project(nc, io, keep, sc, xq, qg, "up")
        keep["w_down"] = buf("w_down", [P, IC, 2, DC, P], F16)
        find_product_peak(nc, io, keep, sc, qg)
        project_down(nc, io, keep, sc, qg)


def build(nc, io):
    def scratch(name, shape, dt):
        return nc.dram_tensor(name + "_dram", shape, dt, kind="Internal").ap()

    io["w_parts"] = scratch("w_parts", (3 * IC, P, 2, DC, P), F16)
    io["x2"] = scratch("x2", (BATCH, SEQ, D), F32)
    io["xt2"] = scratch("xt2", (BATCH, P, DC, SEQ), F32)
    io["gates"] = scratch("gates", (IC, P, TOK), F32)
    io["ups"] = scratch("ups", (IC, P, TOK), F32)
    with ExitStack() as ctx:
        keep = {
            "half": ctx.enter_context(nc.sbuf_tensor("half", [P, 8], F32)),
            "x2_peak": ctx.enter_context(nc.sbuf_tensor("x2_peak", [P, 1], F32)),
        }
        with ExitStack() as first:
            def buf(name, shape, dt):
                keep[name] = first.enter_context(nc.sbuf_tensor(name, shape, dt))

            buf("ident", [P, P], F32)
            buf("ident_b", [P, P], BF16)
            buf("mask", [P, 2 * P], BF16)
            buf("minus_half", [P, TT], F32)
            buf("inv", [P, 8], F32)
            buf("back", [P, 3], F32)
            buf("cos", [P, SEQ], F32)
            buf("sin", [P, SEQ], F32)
            buf("bqk", [P, 2 * DC], F32)
            buf("bv", [P, DC], F32)
            buf("bias_row", [P, D], F32)
            buf("attn_hi", [P, 4, DC, D], F16)
            buf("attn_lo", [P, 4, DC, D], F16)
            prepare(nc, io, keep)
            attend(nc, io, keep)
        feed_forward(nc, io, keep)


def kernel(x, ctx_1024, L0_xattn_Wq, L0_xattn_bq, L0_xattn_Wk, L0_xattn_bk, L0_xattn_Wv, L0_xattn_bv,
           L0_xattn_Wo, L0_xattn_bo, L0_ffn_w_gate, L0_ffn_w_up, L0_ffn_w_down):
    import numpy as np
    import concourse.bacc as bacc
    from concourse.bass_utils import run_bass_kernel_spmd as run

    half = HD // 2
    freq = (1.0 / 10000.0 ** (np.arange(half, dtype=np.float32) / np.float32(half))).astype(np.float32)
    angle = (np.arange(SEQ, dtype=np.float32)[None, :] * freq[:, None]).astype(np.float32)
    cos, sin = np.cos(angle), np.sin(angle)
    heads = P // HD
    units = lambda w: np.asarray(w).reshape(-1, P, D)
    arrays = {
        "x": np.asarray(x),
        "ctx": np.asarray(ctx_1024),
        "attn_w": np.concatenate([units(L0_xattn_Wq), units(L0_xattn_Wk), units(L0_xattn_Wv), units(L0_xattn_Wo)]),
        "ffn_w": np.concatenate([units(L0_ffn_w_gate), units(L0_ffn_w_up),
                                 np.asarray(L0_ffn_w_down).reshape(DC, P, INNER // D, D).transpose(0, 2, 1, 3)
                                 .reshape(IC, P, D)]),
        "bqk": np.concatenate([np.asarray(L0_xattn_bq).reshape(DC, P), np.asarray(L0_xattn_bk).reshape(DC, P)]).T,
        "bv": np.asarray(L0_xattn_bv).reshape(DC, P).T,
        "bias_row": np.broadcast_to(np.asarray(L0_xattn_bo), (P, D)),
        "cos": np.tile(np.concatenate([cos, cos]), (heads, 1)),
        "sin": np.tile(np.concatenate([sin, -sin]), (heads, 1)),
    }
    arrays = {k: np.ascontiguousarray(v) for k, v in arrays.items()}
    nc = bacc.Bacc("TRN2", target_bir_lowering=False, num_devices=1)
    io = {k: nc.dram_tensor(f"in_{k}", v.shape, F32, kind="ExternalInput").ap() for k, v in arrays.items()}
    io["out"] = nc.dram_tensor("out_y", (BATCH, SEQ, D), F32, kind="ExternalOutput").ap()
    build(nc, io)
    r = run(nc, [{f"in_{k}": v for k, v in arrays.items()}], core_ids=[0])
    return r.results[0]["out_y"]
```
